# Optimizing a Trainium2 kernel written in Bass

```python
import numpy as np
import jax
import jax.numpy as jnp

def _softmax(x, axis=-1):
    return jax.nn.softmax(x, axis=axis)

def _gelu(x):
    return jax.nn.gelu(x, approximate=True)

def _silu(x):
    return jax.nn.silu(x)

def _sigmoid(x):
    return jax.nn.sigmoid(x)

def _layernorm(x, axis=-1, eps=1e-05):
    m = jnp.mean(x, axis=axis, keepdims=True)
    v = jnp.var(x, axis=axis, keepdims=True)
    return (x - m) / jnp.sqrt(v + eps)

def _scatter_add(tgt, idx, src, axis=0):
    return tgt.at[idx].add(src)

def _segment_sum(src, seg, n):
    return jax.ops.segment_sum(src, seg, n)
kernel_name = 'mk_seq_preln_d1_jaxref_r8_961147'

def setup_inputs(seed: int=0):
    np.random.seed(seed)
    _w = jnp.asarray

    def _L0_attn_setup():
        import jax, jax.numpy as jnp
        import numpy as np
        import math
        B, S, DM = (1, 256, 512)
        H, HKV, HD = (32, 8, 128)
        EPS = 1e-06
        NEG_INF = -1e+30

        def _alibi_slopes(n_heads: int) -> np.ndarray:
            start = 2 ** (-2 ** (-(math.log2(n_heads) - 3)))
            return np.array([start * start ** i for i in range(n_heads)], dtype=np.float32)

        def _rmsnorm(t, w):
            tf = t.astype(jnp.float32)
            inv = jax.lax.rsqrt(jnp.mean(tf * tf, axis=-1, keepdims=True) + EPS)
            return (tf * inv * w).astype(t.dtype)
        key = jax.random.key(seed)
        ks = jax.random.split(key, 5)
        std = 0.02
        return {'x': jax.random.normal(ks[0], (B, S, DM), dtype=jnp.float32), 'Wq': jax.random.normal(ks[1], (H * HD, DM), dtype=jnp.float32) * std, 'Wk': jax.random.normal(ks[2], (HKV * HD, DM), dtype=jnp.float32) * std, 'Wv': jax.random.normal(ks[3], (HKV * HD, DM), dtype=jnp.float32) * std, 'Wo': jax.random.normal(ks[4], (H * HD, DM), dtype=jnp.float32).T * (std / math.sqrt(2 * 32)), 'q_norm_w': jnp.ones((HD,), dtype=jnp.float32), 'k_norm_w': jnp.ones((HD,), dtype=jnp.float32)}
    _L0_attn_in = _L0_attn_setup()

    def _L0_ffn_setup():
        import jax, jax.numpy as jnp
        import numpy as np
        ALPHA = 32
        R = 16
        SCALING = ALPHA / R
        key = jax.random.key(seed)
        k1, k2, k3, k4 = jax.random.split(key, 4)
        B_, S, D = (4, 256, 512)
        H, r, O = (8, R, 512)
        x = jax.random.normal(k1, (B_, S, D), dtype=jnp.float32)
        A = jax.random.normal(k2, (H, r, D), dtype=jnp.float32) * 0.02
        Bm = jax.random.normal(k3, (H, O, r), dtype=jnp.float32) * 0.02
        Wr = jax.random.normal(k4, (H, D), dtype=jnp.float32) * 0.02
        br = jnp.zeros((H,), dtype=jnp.float32)
        return {'x': x, 'A': A, 'B': Bm, 'Wr': Wr, 'br': br}
    _L0_ffn_in = _L0_ffn_setup()
    _d = {'L0_attn_x': _L0_attn_in['x'], 'L0_attn_Wq': _L0_attn_in['Wq'], 'L0_attn_Wk': _L0_attn_in['Wk'], 'L0_attn_Wv': _L0_attn_in['Wv'], 'L0_attn_Wo': _L0_attn_in['Wo'], 'L0_attn_q_norm_w': _L0_attn_in['q_norm_w'], 'L0_attn_k_norm_w': _L0_attn_in['k_norm_w'], 'L0_ffn_A': _L0_ffn_in['A'], 'L0_ffn_B': _L0_ffn_in['B'], 'L0_ffn_Wr': _L0_ffn_in['Wr'], 'L0_ffn_br': _L0_ffn_in['br']}
    _x0 = _d['L0_attn_x']
    _d['L0_attn_x'] = jax.random.normal(jax.random.fold_in(jax.random.key(seed), 1), (2, 1024, 512), dtype=_x0.dtype)
    del _x0
    return _d

def reference(L0_attn_x, L0_attn_Wq, L0_attn_Wk, L0_attn_Wv, L0_attn_Wo, L0_attn_q_norm_w, L0_attn_k_norm_w, L0_ffn_A, L0_ffn_B, L0_ffn_Wr, L0_ffn_br):

    def _L0_attn_ref(x, Wq, Wk, Wv, Wo, q_norm_w, k_norm_w):
        import jax, jax.numpy as jnp
        import numpy as np
        import math
        B, S, DM = (1, 256, 512)
        H, HKV, HD = (32, 8, 128)
        EPS = 1e-06
        NEG_INF = -1e+30

        def _alibi_slopes(n_heads: int) -> np.ndarray:
            start = 2 ** (-2 ** (-(math.log2(n_heads) - 3)))
            return np.array([start * start ** i for i in range(n_heads)], dtype=np.float32)

        def _rmsnorm(t, w):
            tf = t.astype(jnp.float32)
            inv = jax.lax.rsqrt(jnp.mean(tf * tf, axis=-1, keepdims=True) + EPS)
            return (tf * inv * w).astype(t.dtype)
        b, s, _ = x.shape
        G = H // HKV
        q = (x @ Wq.T).reshape(b, s, H, HD).transpose(0, 2, 1, 3)
        k = (x @ Wk.T).reshape(b, s, HKV, HD).transpose(0, 2, 1, 3)
        v = (x @ Wv.T).reshape(b, s, HKV, HD).transpose(0, 2, 1, 3)
        q = _rmsnorm(q, q_norm_w)
        k = _rmsnorm(k, k_norm_w)
        qg = q.reshape(b, HKV, G, s, HD)
        scores = jnp.einsum('bkgqd,bksd->bkgqs', qg, k) / math.sqrt(HD)
        slopes = jnp.asarray(_alibi_slopes(H)).reshape(HKV, G)
        pos = jnp.arange(s, dtype=jnp.float32)
        rel = pos[None, :] - pos[:, None]
        bias = jnp.where(rel > 0, NEG_INF, slopes[:, :, None, None] * rel)
        attn = jax.nn.softmax(scores + bias[None], axis=-1)
        out = jnp.einsum('bkgqs,bksd->bkgqd', attn, v)
        out = out.reshape(b, H, s, HD).transpose(0, 2, 1, 3).reshape(b, s, H * HD)
        return out @ Wo.T

    def _L0_ffn_ref(x, A, B, Wr, br):
        import jax, jax.numpy as jnp
        import numpy as np
        ALPHA = 32
        R = 16
        SCALING = ALPHA / R
        H = A.shape[0]
        router_logits = jnp.einsum('bsd,hd->bsh', x, Wr) + br
        scores = H * jax.nn.softmax(router_logits, axis=-1)
        low = jnp.einsum('bsd,hrd->bshr', x, A)
        out = jnp.einsum('bshr,hor,bsh->bso', low, B, scores)
        return SCALING * out
    x = L0_attn_x
    x = x + _L0_attn_ref(_layernorm(x, axis=-1), L0_attn_Wq, L0_attn_Wk, L0_attn_Wv, L0_attn_Wo, L0_attn_q_norm_w, L0_attn_k_norm_w)
    x = x + _L0_ffn_ref(_layernorm(x, axis=-1), L0_ffn_A, L0_ffn_B, L0_ffn_Wr, L0_ffn_br)
    return x

_drawn_inputs = setup_inputs


def setup_inputs(seed=0):
    import zlib

    import numpy as np

    out = dict(_drawn_inputs(seed))
    spreads = {'L0_attn_q_norm_w': (1.0, 0.6), 'L0_attn_k_norm_w': (1.0, 0.6), 'L0_ffn_br': (0.0, 0.1)}
    factors = {'L0_attn_Wq': 3.269, 'L0_attn_Wk': 3.268}
    for name, (base, spread) in spreads.items():
        noise = np.random.default_rng([zlib.crc32(name.encode()), seed]).standard_normal(out[name].shape)
        drawn = base * np.exp(spread * noise) if base else spread * noise
        out[name] = jnp.asarray(drawn.astype(out[name].dtype))
    for name, factor in factors.items():
        out[name] = (out[name] * factor).astype(out[name].dtype)
    return out
```

```python
import itertools
import math
from contextlib import ExitStack

import numpy as np

import concourse.bass as bass
from concourse import mybir

ALU = mybir.AluOpType
ACT = mybir.ActivationFunctionType
F32 = mybir.dt.float32
F32R = mybir.dt.float32r

P = 128
LN_EPS = 1e-5
RMS_EPS = 1e-6
NEG_INF = -1e30
LORA_SCALING = 32 / 16
BIG = 3e38


def alibi_slopes(n_heads):
    start = 2 ** (-2 ** (-(math.log2(n_heads) - 3)))
    return np.array([start * start ** i for i in range(n_heads)], dtype=np.float32)


def attention_lora_block(nc, x, Wq, Wk, Wv, Wo, q_norm_w, k_norm_w, A, B, Wr, br, out):
    NB, S, DM = x.shape
    HD = q_norm_w.shape[0]
    H = Wq.shape[0] // HD
    NG = Wk.shape[0] // HD
    G = H // NG
    NE, RK, _ = A.shape
    NT = S // P
    C = DM // P
    W512 = G * HD
    assert HD == P and W512 == 512 and DM == 512 and NE * RK == P and S == 1024
    slopes = alibi_slopes(H)
    CARRIERS = 16
    RING = 3
    LAG = RING - 1

    def q_parts(s):
        return [("q_part", s, c) for c in range(C)] + [("square_q", s), ("inv_q", s)]

    def step(s, following):
        more_q = range(1, NT + 2 if following else NT)
        n = s
        turn = [("turn", "p", s - 1, j) for j in range(n)]
        value = [("values", s - 1, j) for j in range(n)]
        middle = [[turn[j + LAG], value[j]] for j in range(n - LAG)]
        last = value[max(0, n - LAG):]
        m = len(middle)
        cuts = [0, (m + 2) // 3, (2 * m + 2) // 3, m]
        part = [sum(middle[cuts[i]:cuts[i + 1]], []) for i in range(3)]
        weights = [[], [], [], []]
        if s == 0:
            weights = [[("turn", "wo", 0), ("turn", "wo", 1)], [("turn", "wo", 2)], [("turn", "wo", 3)], []]
        if s == NT - 2 and following:
            weights = [[("turn", "wkv", 0)], [("turn", "wkv", 1), ("turn", "wq", 0)], [("turn", "wq", 1), ("turn", "wq", 2)],
                       [("turn", "wq", 3)]]
        plan = [("scores", s, 0)]
        plan += [("y", s - 2)] if s >= 2 else []
        plan += weights[0] + [("exp", s, 0)] + turn[:LAG]
        plan += [("scores", s, 1)]
        plan += ([("norm_q", s + 1)] if s + 1 in more_q else []) + part[0][:2] + [("exp", s, 1)] + weights[1] + part[0][2:]
        plan += [("scores", s, 2), ("invert", s, 0)]
        plan += ([("turn", "q", s + 1)] if s + 1 in more_q else []) + part[1][:2] + weights[2] + [("exp", s, 2)]
        plan += [("normalise", s, 0), ("normalise", s, 1)] + part[1][2:]
        plan += [("scores", s, 3)] + part[2][:2] + weights[3] + [("exp", s, 3)] + part[2][2:]
        q = q_parts(s + 2) if s + 2 in more_q and s + 2 < NT + 2 - (s == NT - 1) else []
        fill = q[:1] if last else []
        for v in last:
            plan += fill + [v]
            q, fill = q[len(fill):], q[len(fill):len(fill) + 1]
        plan += q + [("invert", s, 1), ("normalise", s, 2), ("normalise", s, 3)]
        return plan

    def tail(following):
        n, s = NT, NT - 1
        turn = [("turn", "p", s, j) for j in range(n)]
        value = [("values", s, j) for j in range(n)]
        pair = [[turn[j + LAG], value[j]] for j in range(n - LAG)]
        if not following:
            return [("y", NT - 2)] + turn[:LAG] + sum(pair, []) + value[n - LAG:] + [("y", NT - 1)]
        plan = [("y", NT - 2), ("kv", 0)] + turn[:LAG] + [("kv", 1)] + pair[0] + pair[1] + [("kv", 2)]
        plan += pair[2] + [("kv", 3), ("inv_k",)] + pair[3] + [("table", 0)] + pair[4] + pair[5]
        plan += [("norm_k",), ("turn", "k", 0), value[n - 2], ("turn", "k", 1), value[n - 1], ("split_v",)]
        return plan + q_parts(NT + 1) + [("table", 1), ("y", NT - 1), ("table", 2), ("table", 3)]

    PREPARE = ([("turn", "wkv", i) for i in range(C // 2)] + [("turn", "wq", c) for c in range(C)]
               + [("table", 0)] + [("kv", i) for i in range(NT // 2)] + [("inv_k",)] + q_parts(NT)
               + [("norm_k",), ("turn", "k", 0), ("turn", "k", 1), ("split_v",), ("norm_q", NT), ("turn", "q", NT)]
               + q_parts(NT + 1) + [("table", h) for h in range(1, G)])
    GROUP = sum((step(s, True) for s in range(NT)), []) + tail(True)
    LAST_GROUP = sum((step(s, False) for s in range(NT)), []) + tail(False)

    UNIT_X, UNIT_LOW, n = {}, {}, 0
    for i in range(NT + 3):
        if i < NT:
            UNIT_X[i], n = n, n + 1
        if 0 <= i - 3 < NT:
            UNIT_LOW[i - 3], n = n, n + 1

    def signals(kind):
        return tuple(sum(x[0] == kind for x in plan) for plan in (PREPARE, GROUP, LAST_GROUP))

    q_counts = tuple(sum(x[0] == "q_part" and x[2] == C - 1 for x in plan) for plan in (PREPARE, GROUP, LAST_GROUP))
    COUNTS = {
        "turned": (3, NT, *signals("turn"), 2 * NT),
        "hi_done": (0, NT, *signals("turn"), 0),
        "lo_done": (3, NT, *signals("turn"), 2 * NT),
        "ln_stats": (0, NT, 0, 0, 0, NT), "ln_moments": (0, NT, 0, 0, 0, NT), "ln_var_eps": (0, 2, 0, 0, 0, 2),
        "ln_rstd": (0, 2, 0, 0, 0, 2), "xn_ready": (0, NT, 0, 0, 0, NT),
        "bias_ready": (0, 0, *signals("table"), 0),
        "kv_full": (0, 0, *signals("kv"), 0), "kv_squares": (0, 0, *signals("kv"), 0),
        "kv_copied": (0, 0, *signals("kv"), 0),
        "k_sum_eps": (0, 0, *signals("inv_k"), 0), "k_inv": (0, 0, *signals("inv_k"), 0),
        "k_normed": (0, 0, *signals("norm_k"), 0),
        "v_hi_done": (0, 0, *signals("split_v"), 0), "v_lo_done": (0, 0, *signals("split_v"), 0),
        "q_full": (0, 0, *q_counts, 0), "q_squares": (0, 0, *q_counts, 0), "q_sum_eps": (0, 0, *q_counts, 0),
        "q_inv": (0, 0, *q_counts, 0), "q_normed": (0, 0, *signals("norm_q"), 0),
        "s_full": (0, 0, *signals("scores"), 0), "s_max": (0, 0, *signals("scores"), 0),
        "p_exp": (0, 0, *signals("exp"), 0), "p_inv": (0, 0, *signals("invert"), 0),
        "p_ready": (0, 0, *signals("normalise"), 0),
        "o_full": (0, 0, *signals("y"), 0), "o_hi": (0, 0, *signals("y"), 0), "o_lo": (0, 0, *signals("y"), 0),
        "y_full": (0, 0, *signals("y"), 0), "y_added": (0, 0, *signals("y"), 0),
        "f_full": (0, 0, 0, 0, 0, NT), "f_max": (0, 0, 0, 0, 0, NT), "f_exp": (0, 0, 0, 0, 0, NT),
        "f_inv": (0, 0, 0, 0, 0, NT), "f_gate": (0, 0, 0, 0, 0, NT), "f_low": (0, 0, 0, 0, 0, NT),
        "f_out": (0, 0, 0, 0, 0, NT), "f_added": (0, 0, 0, 0, 0, NT),
    }

    def batch_at(name, b):
        pro, ln, prep, grp, last, ffn = COUNTS[name]
        return b * (ln + prep + (NG - 1) * grp + last + ffn) + pro

    def ln_at(name, b):
        return batch_at(name, b)

    def prepare_at(name, b):
        return batch_at(name, b) + COUNTS[name][1]

    def group_at(name, b, g):
        pro, ln, prep, grp, last, ffn = COUNTS[name]
        return batch_at(name, b) + g * grp + (ln + prep)

    def ffn_at(name, b):
        pro, ln, prep, grp, last, ffn = COUNTS[name]
        return batch_at(name, b) + (ln + prep + (NG - 1) * grp + last)

    def units(plan):
        return {x[1:]: n for n, x in enumerate(x for x in plan if x[0] == "turn")}

    def piece(s, j):
        return s * (s + 1) // 2 + j

    def follow(work, plan):
        for kind, *what in plan:
            if kind in work:
                work[kind](*what)

    with ExitStack() as ctx:
        def sb(name, shape, dt=F32):
            return ctx.enter_context(nc.sbuf_tensor(name, shape, dt))

        def psum(name, shape):
            return ctx.enter_context(nc.psum_tensor(name, shape, F32))

        def sem(name):
            return ctx.enter_context(nc.semaphore(name))

        xnT_hi = sb("xnT_hi", [P, C, S], F32R)
        xnT_lo = sb("xnT_lo", [P, C, S], F32R)
        y = sb("y", [P, NT, DM])
        wqT_hi = sb("wqT_hi", [P, C, W512], F32R)
        wqT_lo = sb("wqT_lo", [P, C, W512], F32R)
        wkvT_hi = sb("wkvT_hi", [P, C, 2 * HD], F32R)
        wkvT_lo = sb("wkvT_lo", [P, C, 2 * HD], F32R)
        woT_hi = sb("woT_hi", [P, G, DM], F32R)
        woT_lo = sb("woT_lo", [P, G, DM], F32R)
        wq_raw = sb("wq_raw", [P, G, DM])
        wkv_raw = sb("wkv_raw", [P, 2, DM])
        wo_raw = sb("wo_raw", [P, C, W512])
        kT_hi = sb("kT_hi", [P, S], F32R)
        kT_lo = sb("kT_lo", [P, S], F32R)
        v_hi = sb("v_hi", [P, NT, HD], F32R)
        v_lo = sb("v_lo", [P, NT, HD], F32R)
        rel = sb("rel", [P, S])
        bias = sb("bias", [P, G, S])
        probs = sb("probs", [P, 2, G, S])
        qn = sb("qn", [P, G, HD])
        qT_hi = sb("qT_hi", [P, 2, G, P], F32R)
        qT_lo = sb("qT_lo", [P, 2, G, P], F32R)
        pT_hi = sb("pT_hi", [P, RING, G * P], F32R)
        pT_lo = sb("pT_lo", [P, RING, G * P], F32R)
        oT_hi = sb("oT_hi", [P, G, P], F32R)
        oT_lo = sb("oT_lo", [P, G, P], F32R)
        arT = sb("arT", [P, C, P + NE])
        bT = sb("bT", [P, DM])
        ident = sb("ident", [P, P])
        slope_row = sb("slope_row", [P, H])
        minus_half = sb("minus_half", [P, NT])
        ln_eps = sb("ln_eps", [P, NT // 2])
        rms_eps = sb("rms_eps", [P, NT])
        scratch = sb("scratch", [P, CARRIERS, 1])
        wq_norm = sb("wq_norm", [P, 1])
        wk_norm = sb("wk_norm", [P, 1])
        wk_scaled = sb("wk_scaled", [P, 1])
        br_row = sb("br_row", [P, NE])
        stats = sb("stats", [P, NT, 6])
        moments = sb("moments", [P, NT, 2])
        var_eps = sb("var_eps", [P, NT])
        rstd = sb("rstd", [P, NT])
        k_sum = sb("k_sum", [P, NT])
        k_sum_eps_t = sb("k_sum_eps_t", [P, NT])
        k_inv_t = sb("k_inv_t", [P, NT])
        q_sum = sb("q_sum", [P, G])
        q_sum_eps_t = sb("q_sum_eps_t", [P, G])
        q_inv_t = sb("q_inv_t", [P, G])
        neg_max = sb("neg_max", [P, 2, G])
        p_sum = sb("p_sum", [P, 2, G])
        p_inv_t = sb("p_inv_t", [P, 2, G])
        f_neg_max = sb("f_neg_max", [P, NT])
        f_sum = sb("f_sum", [P, NT])
        f_inv_t = sb("f_inv_t", [P, NT])

        slots = probs[:].rearrange("p a h s -> p (a h) s")
        kv_raw = probs[:, 0, 0:2, :].rearrange("p a (t d) -> p (a t) d", d=2 * HD)
        k_norm = probs[:, 0, 2, :].rearrange("p (t d) -> p t d", d=HD)
        x_normed = slots[:, :, 0:DM]
        x_turned = slots[:, :, DM:2 * DM]
        low_gated = bias[:, 0, :].rearrange("p (t n) -> p t n", n=P)
        low_turned = bias[:, 1, :].rearrange("p (t n) -> p t n", n=P)
        a_raw = slots[:, 0, 0:DM]
        wr_raw = slots[0:NE, 1, 0:DM]
        b_raw = slots[:, 2, 0:DM].rearrange("p (o h r) -> p o h r", o=C, r=RK)
        f_logits, f_weights, f_gates = (
            bias[:, 2, i * NT * NE:(i + 1) * NT * NE].rearrange("p (t n) -> p t n", n=NE) for i in range(3))

        s_ps = psum("s_ps", [P, 1024])
        turn_ps = [psum(f"turn_ps{i}", [P, 512]) for i in range(RING)]
        q_ps = psum("q_ps", [P, 512])
        o_ps = psum("o_ps", [P, 512])
        y_ps = psum("y_ps", [P, 512])

        sems = {name: sem(name) for name in COUNTS}
        ident_ready = sem("ident_ready")
        rel_ready = sem("rel_ready")
        tables_ready = sem("tables_ready")
        wk_scaled_ready = sem("wk_scaled_ready")
        pool_step = sem("pool_step")
        small_loaded = sem("small_loaded")
        ffn_loaded = sem("ffn_loaded")
        x_loaded = [sem(f"x_loaded{i}") for i in range(NT // 2)]
        wkv_loaded = sem("wkv_loaded")
        wq_loaded = sem("wq_loaded")
        wo_loaded = sem("wo_loaded")
        stored = sem("stored")

        block = ctx.enter_context(nc.Block())

        def run_plans(engine, run, b, with_group=False):
            def prepared(name):
                return prepare_at(name, b) + (COUNTS[name][2] - COUNTS[name][3])

            run(PREPARE, prepared, lambda name: prepare_at(name, b), *([0] if with_group else []))
            with engine.Fori(0, NG - 1) as g:
                run(GROUP, lambda name: group_at(name, b, g), lambda name: group_at(name, b, g),
                    *([g + 1] if with_group else []))
            run(LAST_GROUP, lambda name: group_at(name, b, NG - 1), lambda name: group_at(name, b, NG - 1),
                *([NG - 1] if with_group else []))

        @block.sync
        def _(sp):
            x_v = x.rearrange("b (t p) d -> b p t d", p=P)
            out_v = out.rearrange("b (t p) d -> b p t d", p=P)
            wq_v = Wq.rearrange("(g h p) d -> g p h d", h=G, p=P)
            wk_v = Wk.rearrange("(g p) d -> g p d", p=P)
            wv_v = Wv.rearrange("(g p) d -> g p d", p=P)
            wo_v = Wo.rearrange("(c p) (g n) -> g p c n", p=P, n=W512)

            def load_wqkv(g):
                sp.dma_start(wkv_raw[:, 0, :], wk_v[g]).then_inc(wkv_loaded, 16)
                sp.dma_start(wkv_raw[:, 1, :], wv_v[g]).then_inc(wkv_loaded, 16)
                sp.dma_start(wq_raw[:], wq_v[g]).then_inc(wq_loaded, 16)

            def load_wo(g):
                sp.dma_start(wo_raw[:], wo_v[g]).then_inc(wo_loaded, 16)

            wo_turned = units(GROUP)["wo", G - 1] + 1

            def load_next(b, g, following):
                sp.wait_ge(sems["turned"], group_at("turned", b, g))
                load_wqkv(following)
                sp.wait_ge(sems["turned"], group_at("turned", b, g) + wo_turned)
                load_wo(following)

            def load_x(b):
                for i in range(NT // 2):
                    sp.dma_start(y[:, 2 * i:2 * i + 2, :], x_v[b, :, 2 * i:2 * i + 2, :]).then_inc(x_loaded[i], 16)

            def store(b):
                for t in range(NT):
                    sp.wait_ge(sems["f_added"], ffn_at("f_added", b) + t + 1)
                    sp.dma_start(out_v[b, :, t, :], y[:, t, :]).then_inc(stored, 16)

            load_x(0)
            load_wqkv(0)
            load_wo(0)
            for b in range(NB):
                with sp.Fori(0, NG - 1) as g:
                    load_next(b, g, g + 1)
                if b < NB - 1:
                    load_next(b, NG - 1, 0)
                store(b)
                sp.wait_ge(stored, 16 * NT * (b + 1))
                if b < NB - 1:
                    load_x(b + 1)

        @block.scalar
        def _(act):
            act.dma_start(a_raw, A.rearrange("h r d -> (h r) d")).then_inc(ffn_loaded, 16)
            act.dma_start(wr_raw, Wr).then_inc(ffn_loaded, 16)
            for o in range(C):
                act.dma_start(b_raw[:, o], B.rearrange("h (o p) r -> o p h r", p=P)[o]).then_inc(ffn_loaded, 16)
            act.dma_start(wq_norm[:], q_norm_w.rearrange("(p a) -> p a", a=1)).then_inc(small_loaded, 16)
            act.dma_start(wk_norm[:], k_norm_w.rearrange("(p a) -> p a", a=1)).then_inc(small_loaded, 16)
            act.dma_start(br_row[:], br.rearrange("(a n) -> a n", a=1).broadcast_to((P, NE))).then_inc(small_loaded, 16)
            act.wait_ge(small_loaded, 48)
            act.wait_ge(wk_scaled_ready, 1)

            def high(base, unit, target, source, scale=None):
                act.wait_ge(sems["turned"], base + unit + 1)
                if scale is None:
                    nc.scalar.activation(target, source, ACT.Copy).then_inc(sems["hi_done"], 1)
                else:
                    nc.scalar.activation(target, source, ACT.Copy, scale=scale).then_inc(sems["hi_done"], 1)

            with act.Fori(0, NB) as b:
                base = ln_at("turned", b)
                for t in range(NT):
                    high(base, t, xnT_hi[:, :, t * P:(t + 1) * P],
                         turn_ps[t % RING][:].rearrange("p (c n) -> p c n", c=C))

                def run(plan, at, start):
                    unit_of = units(plan)
                    base = start("turned")

                    def turn(what, *which):
                        unit = unit_of[(what, *which)]
                        bank = turn_ps[unit % RING][:]
                        if what == "p":
                            high(base, unit, pT_hi[:, piece(*which) % RING, :], bank)
                        elif what == "q":
                            high(base, unit, qT_hi[:, which[0] % 2].rearrange("p h n -> p (h n)"), bank, wq_norm[:])
                        elif what == "k":
                            high(base, unit, kT_hi[:, which[0] * 512:(which[0] + 1) * 512], bank, wk_scaled[:])
                        elif what == "wkv":
                            i = which[0]
                            high(base, unit, wkvT_hi[:, 2 * i:2 * i + 2, :].rearrange("p c n -> p (c n)"), bank)
                        elif what == "wq":
                            high(base, unit, wqT_hi[:, which[0], :], bank)
                        elif what == "wo":
                            high(base, unit, woT_hi[:, which[0], :], bank)

                    def exp(s, h):
                        n = s * G + h
                        L = (s + 1) * P
                        act.wait_ge(sems["s_max"], at("s_max") + n + 1)
                        row = probs[:, s % 2, h, 0:L]
                        nc.scalar.activation(row, row, ACT.Exp, bias=neg_max[:, s % 2, h:h + 1], scale=-1.0,
                                             accum_out=p_sum[:, s % 2, h:h + 1]).then_inc(sems["p_exp"], 1)

                    def square_q(s):
                        act.wait_ge(sems["q_full"], at("q_full") + s - 1)
                        for h in range(G):
                            last = nc.scalar.activation(qn[:, h, :], q_ps[:, h * HD:(h + 1) * HD], ACT.Square,
                                                        accum_out=q_sum[:, h:h + 1])
                        last.then_inc(sems["q_squares"], 1)

                    def kv(i):
                        act.wait_ge(sems["kv_full"], start("kv_full") + i + 1)
                        for t in range(2):
                            last = nc.scalar.activation(k_norm[:, 2 * i + t, :], s_ps[:, 512 * (i % 2) + t * 2 * HD:][:, 0:HD],
                                                        ACT.Square, accum_out=k_sum[:, 2 * i + t:2 * i + t + 1])
                        last.then_inc(sems["kv_squares"], 1)

                    def split_v():
                        act.wait_ge(sems["kv_copied"], start("kv_copied") + NT // 2)
                        if plan is GROUP:
                            act.wait_ge(sems["o_full"], at("o_full") + NT)
                        nc.scalar.activation(v_hi[:], kv_raw[:, :, HD:2 * HD], ACT.Copy).then_inc(sems["v_hi_done"], 1)

                    def values(s, j):
                        if j == s:
                            act.wait_ge(sems["o_full"], at("o_full") + s + 1)
                            nc.scalar.activation(oT_hi[:].rearrange("p h n -> p (h n)"), o_ps[:],
                                                 ACT.Copy).then_inc(sems["o_hi"], 1)

                    follow({"turn": turn, "exp": exp, "square_q": square_q, "kv": kv, "split_v": split_v,
                            "values": values}, plan)

                run_plans(act, run, b)
                for t in range(NT):
                    act.wait_ge(sems["f_max"], ffn_at("f_max", b) + t + 1)
                    nc.scalar.activation(f_weights[:, t, :], f_logits[:, t, :], ACT.Exp, bias=f_neg_max[:, t:t + 1],
                                         scale=-1.0, accum_out=f_sum[:, t:t + 1]).then_inc(sems["f_exp"], 1)

        @block.gpsimd
        def _(pool):
            nc.gpsimd.memset(ident[:], 0.0).then_inc(pool_step, 1)
            nc.gpsimd.iota(rel[:], [[1, S]], base=-(S - P), channel_multiplier=-1,
                           allow_small_or_imprecise_dtypes=True).then_inc(pool_step, 1)
            pool.wait_ge(pool_step, 2)
            nc.gpsimd.affine_select(out=ident[:], in_=ident[:], compare_op=ALU.not_equal, fill=1.0, base=0,
                                    pattern=[[-1, P]], channel_multiplier=1).then_inc(ident_ready, 1)
            nc.gpsimd.affine_select(out=rel[:], in_=rel[:], compare_op=ALU.is_ge, fill=NEG_INF, base=S - P,
                                    pattern=[[-1, S]], channel_multiplier=1).then_inc(rel_ready, 1)
            pool.wait_ge(rel_ready, 1)
            pool.wait_ge(tables_ready, 1)

            def inverse_root(base_eps, target, eps_t, source, eps, n, name_eps, name_out):
                nc.gpsimd.tensor_tensor(eps_t, source, eps, ALU.add).then_inc(sems[name_eps], 1)
                pool.wait_ge(sems[name_eps], base_eps + 1)
                nc.gpsimd.tensor_tensor(target, eps_t, minus_half[:, 0:n], ALU.pow).then_inc(sems[name_out], 1)

            def layer_norm(at):
                half = NT // 2
                for i in range(2):
                    r = slice(i * half, (i + 1) * half)
                    pool.wait_ge(sems["ln_moments"], at("ln_moments") + half * (i + 1))
                    inverse_root(at("ln_var_eps") + i, rstd[:, r], var_eps[:, r], moments[:, r, 1], ln_eps[:], half,
                                 "ln_var_eps", "ln_rstd")

            with pool.Fori(0, NB) as b:
                layer_norm(lambda name: ln_at(name, b))

                def run(plan, at, start, g):
                    def inv_q(s):
                        n = at("q_sum_eps") + s - 2
                        pool.wait_ge(sems["q_squares"], at("q_squares") + s - 1)
                        inverse_root(n, q_inv_t[:], q_sum_eps_t[:], q_sum[:], rms_eps[:, 0:G], G, "q_sum_eps", "q_inv")

                    def inv_k():
                        pool.wait_ge(sems["kv_squares"], start("kv_squares") + NT // 2)
                        inverse_root(start("k_sum_eps"), k_inv_t[:], k_sum_eps_t[:], k_sum[:], rms_eps[:], NT,
                                     "k_sum_eps", "k_inv")

                    def normalise(s, h):
                        L = (s + 1) * P
                        if h % 2 == 0:
                            pool.wait_ge(sems["p_inv"], at("p_inv") + 2 * s + h // 2 + 1)
                        row = probs[:, s % 2, h, 0:L]
                        nc.gpsimd.tensor_tensor(row, row, p_inv_t[:, s % 2, h:h + 1].to_broadcast((P, L)),
                                                ALU.mult).then_inc(sems["p_ready"], 1)

                    def table(h):
                        if h == 0:
                            pool.wait_ge(sems["turned"], start("turned") + 1)
                        if plan is GROUP:
                            pool.wait_ge(sems["s_max"], at("s_max") + (NT - 1) * G + h + 1)
                        nc.gpsimd.tensor_tensor(bias[:, h, :], rel[:],
                                                slope_row[:, bass.ds(g * G + h, 1)].to_broadcast((P, S)),
                                                ALU.mult).then_inc(sems["bias_ready"], 1)

                    follow({"inv_q": inv_q, "inv_k": inv_k, "normalise": normalise, "table": table}, plan)

                run_plans(pool, run, b, True)
                layer_norm(lambda name: ffn_at(name, b))

        @block.vector
        def _(dve):
            nc.vector.memset(minus_half[:], -0.5)
            nc.vector.memset(ln_eps[:], LN_EPS)
            nc.vector.memset(rms_eps[:], HD * RMS_EPS)
            for h in range(H):
                last = nc.vector.memset(slope_row[:, h:h + 1], float(slopes[h]))
            last.then_inc(tables_ready, 1)
            dve.wait_ge(small_loaded, 48)

            carriers = itertools.count()

            def alone():
                nc.vector.memset(scratch[:, next(carriers) % CARRIERS, :], 0.0)

            nc.vector.tensor_scalar(wk_scaled[:], wk_norm[:], math.sqrt(HD), None, ALU.mult).then_inc(wk_scaled_ready, 1)
            dve.wait_ge(wk_scaled_ready, 1)

            dve.wait_ge(sems["turned"], 1)
            nc.vector.tensor_copy(arT[:, :, 0:P], turn_ps[0][:].rearrange("p (c n) -> p c n", c=C)).then_inc(sems["lo_done"], 1)
            dve.wait_ge(sems["turned"], 2)
            nc.vector.tensor_copy(arT[:, :, P:P + NE], turn_ps[1][:, 0:C * NE].rearrange("p (c n) -> p c n", c=C)).then_inc(sems["lo_done"], 1)
            dve.wait_ge(sems["turned"], 3)
            nc.vector.tensor_copy(bT[:], turn_ps[2][:]).then_inc(sems["lo_done"], 1)

            def layer_norm(at, ready):
                half = NT // 2
                for i in range(2):
                    for t in range(i * half, (i + 1) * half):
                        ready(t)
                        nc.vector.bn_stats(stats[:, t, :], y[:, t, :]).then_inc(sems["ln_stats"], 1)
                    for t in range(i * half, (i + 1) * half):
                        dve.wait_ge(sems["ln_stats"], at("ln_stats") + t + 1)
                        alone()
                        nc.vector.bn_aggr(moments[:, t, :], stats[:, t, :]).then_inc(sems["ln_moments"], 1)
                for t in range(NT):
                    if t % half == 0:
                        dve.wait_ge(sems["ln_rstd"], at("ln_rstd") + t // half + 1)
                    nc.vector.tensor_scalar(x_normed[:, t, :], y[:, t, :], moments[:, t, 0:1], rstd[:, t:t + 1],
                                            ALU.subtract, ALU.mult).then_inc(sems["xn_ready"], 1)

            def low(base, unit, target, source, high, scale=None):
                dve.wait_ge(sems["hi_done"], base + unit + 1)
                if scale is None:
                    nc.vector.tensor_tensor(target, source, high.bitcast(F32), ALU.subtract).then_inc(sems["lo_done"], 1)
                else:
                    nc.vector.scalar_tensor_tensor(target, source, scale, high.bitcast(F32), ALU.mult,
                                                   ALU.subtract).then_inc(sems["lo_done"], 1)

            with dve.Fori(0, NB) as b:
                def x_ready(t):
                    if t % 2 == 0:
                        dve.wait_ge(x_loaded[t // 2], b * 16 + 16)

                layer_norm(lambda name: ln_at(name, b), x_ready)
                base = ln_at("hi_done", b)
                for t in range(NT):
                    cols = slice(t * P, (t + 1) * P)
                    low(base, t, xnT_lo[:, :, cols], turn_ps[t % RING][:].rearrange("p (c n) -> p c n", c=C),
                        xnT_hi[:, :, cols])

                def run(plan, at, start):
                    unit_of = units(plan)
                    base = start("hi_done")

                    def turn(what, *which):
                        unit = unit_of[(what, *which)]
                        bank = turn_ps[unit % RING][:]
                        if what == "p":
                            r = piece(*which) % RING
                            low(base, unit, pT_lo[:, r, :], bank, pT_hi[:, r, :])
                        elif what == "q":
                            flat = "p h n -> p (h n)"
                            low(base, unit, qT_lo[:, which[0] % 2].rearrange(flat), bank, qT_hi[:, which[0] % 2].rearrange(flat),
                                wq_norm[:])
                        elif what == "k":
                            cols = slice(which[0] * 512, (which[0] + 1) * 512)
                            low(base, unit, kT_lo[:, cols], bank, kT_hi[:, cols], wk_scaled[:])
                        elif what == "wkv":
                            chunks = slice(2 * which[0], 2 * which[0] + 2)
                            low(base, unit, wkvT_lo[:, chunks, :].rearrange("p c n -> p (c n)"), bank,
                                wkvT_hi[:, chunks, :].rearrange("p c n -> p (c n)"))
                        elif what == "wq":
                            low(base, unit, wqT_lo[:, which[0], :], bank, wqT_hi[:, which[0], :])
                        elif what == "wo":
                            low(base, unit, woT_lo[:, which[0], :], bank, woT_hi[:, which[0], :])

                    def scores(s, h):
                        n = s * G + h
                        L = (s + 1) * P
                        if s == 0:
                            dve.wait_ge(sems["bias_ready"], at("bias_ready") - G + h + 1)
                        dve.wait_ge(sems["s_full"], at("s_full") + n + 1)
                        alone()
                        at_col = 512 * (h % 2) if L <= 512 else 0
                        nc.vector.tensor_tensor_reduce(
                            out=probs[:, s % 2, h, 0:L], in0=s_ps[:, at_col:at_col + L], in1=bias[:, h, S - L:S],
                            scale=-1.0, scalar=BIG, op0=ALU.add, op1=ALU.min,
                            accum_out=neg_max[:, s % 2, h:h + 1]).then_inc(sems["s_max"], 1)

                    def invert(s, i):
                        n = s * G + 2 * i + 1
                        dve.wait_ge(sems["p_exp"], at("p_exp") + n + 1)
                        nc.vector.reciprocal(p_inv_t[:, s % 2, 2 * i:2 * i + 2],
                                             p_sum[:, s % 2, 2 * i:2 * i + 2]).then_inc(sems["p_inv"], 1)

                    def norm_q(s):
                        dve.wait_ge(sems["q_inv"], at("q_inv") + s - 1)
                        nc.vector.tensor_tensor(qn[:], q_ps[:].rearrange("p (h d) -> p h d", h=G),
                                                q_inv_t[:].unsqueeze(2).to_broadcast((P, G, HD)),
                                                ALU.mult).then_inc(sems["q_normed"], 1)

                    def kv(i):
                        dve.wait_ge(sems["kv_squares"], start("kv_squares") + i + 1)
                        nc.vector.tensor_copy(kv_raw[:, 2 * i:2 * i + 2, :],
                                              s_ps[:, 512 * (i % 2):512 * (i % 2 + 1)].rearrange("p (t n) -> p t n", t=2))\
                            .then_inc(sems["kv_copied"], 1)

                    def norm_k():
                        dve.wait_ge(sems["kv_copied"], start("kv_copied") + NT // 2)
                        dve.wait_ge(sems["k_inv"], start("k_inv") + 1)
                        nc.vector.tensor_tensor(k_norm[:], kv_raw[:, :, 0:HD],
                                                k_inv_t[:].unsqueeze(2).to_broadcast((P, NT, HD)),
                                                ALU.mult).then_inc(sems["k_normed"], 1)

                    def split_v():
                        dve.wait_ge(sems["v_hi_done"], start("v_hi_done") + 1)
                        nc.vector.tensor_tensor(v_lo[:], kv_raw[:, :, HD:2 * HD], v_hi[:].bitcast(F32),
                                                ALU.subtract).then_inc(sems["v_lo_done"], 1)

                    def values(s, j):
                        if j == s:
                            dve.wait_ge(sems["o_hi"], at("o_hi") + s + 1)
                            nc.vector.tensor_tensor(oT_lo[:].rearrange("p h n -> p (h n)"), o_ps[:],
                                                    oT_hi[:].rearrange("p h n -> p (h n)").bitcast(F32),
                                                    ALU.subtract).then_inc(sems["o_lo"], 1)

                    def add_y(s):
                        dve.wait_ge(sems["y_full"], at("y_full") + s + 1)
                        nc.vector.tensor_tensor(y[:, s, :], y_ps[:], y[:, s, :], ALU.add).then_inc(sems["y_added"], 1)

                    follow({"turn": turn, "scores": scores, "invert": invert, "norm_q": norm_q, "kv": kv, "norm_k": norm_k,
                            "split_v": split_v, "values": values, "y": add_y}, plan)

                run_plans(dve, run, b)

                def fat(name):
                    return ffn_at(name, b)

                def y_ready(t):
                    if t == 0:
                        dve.wait_ge(sems["y_added"], fat("y_added"))

                layer_norm(fat, y_ready)
                for i in range(NT + 4):
                    if i < NT:
                        dve.wait_ge(sems["turned"], fat("turned") + UNIT_X[i] + 1)
                        nc.vector.tensor_copy(x_turned[:, i, :], turn_ps[UNIT_X[i] % RING][:]).then_inc(sems["lo_done"], 1)
                    if 0 <= i - 1 < NT:
                        t = i - 1
                        dve.wait_ge(sems["f_full"], fat("f_full") + t + 1)
                        alone()
                        nc.vector.tensor_tensor_reduce(
                            out=f_logits[:, t, :], in0=(q_ps, o_ps)[t % 2][:, P:P + NE], in1=br_row[:], scale=-1.0,
                            scalar=BIG, op0=ALU.add, op1=ALU.min, accum_out=f_neg_max[:, t:t + 1]).then_inc(sems["f_max"], 1)
                    if 0 <= i - 2 < NT:
                        t = i - 2
                        dve.wait_ge(sems["f_exp"], fat("f_exp") + t + 1)
                        nc.vector.reciprocal(f_inv_t[:, t:t + 1], f_sum[:, t:t + 1]).then_inc(sems["f_inv"], 1)
                        dve.wait_ge(sems["f_inv"], fat("f_inv") + t + 1)
                        nc.vector.tensor_scalar(f_gates[:, t, :], f_weights[:, t, :], f_inv_t[:, t:t + 1],
                                                NE * LORA_SCALING, ALU.mult, ALU.mult).then_inc(sems["f_gate"], 1)
                        dve.wait_ge(sems["f_gate"], fat("f_gate") + t + 1)
                        nc.vector.tensor_tensor(low_gated[:, t, :].rearrange("p (h r) -> p h r", r=RK),
                                                (q_ps, o_ps)[t % 2][:, 0:P].rearrange("p (h r) -> p h r", r=RK),
                                                f_gates[:, t, :].unsqueeze(2).to_broadcast((P, NE, RK)),
                                                ALU.mult).then_inc(sems["f_low"], 1)
                    if 0 <= i - 3 < NT:
                        t = i - 3
                        dve.wait_ge(sems["turned"], fat("turned") + UNIT_LOW[t] + 1)
                        nc.vector.tensor_copy(low_turned[:, t, :], turn_ps[UNIT_LOW[t] % RING][:, 0:P]).then_inc(sems["lo_done"], 1)
                    if 0 <= i - 4 < NT:
                        t = i - 4
                        dve.wait_ge(sems["f_out"], fat("f_out") + t + 1)
                        nc.vector.tensor_tensor(y[:, t, :], y_ps[:], y[:, t, :], ALU.add).then_inc(sems["f_added"], 1)

        @block.tensor
        def _(pe):
            def turn(base, unit, sources, start_free=None):
                if base is not None:
                    pe.wait_ge(sems["lo_done"], base + max(0, unit - RING + 1))
                width = sources[0].shape[0]
                for i, source in enumerate(sources):
                    last = nc.tensor.transpose(turn_ps[unit % RING][0:source.shape[1], i * width:(i + 1) * width],
                                               source, ident[0:width, 0:width])
                last.then_inc(sems["turned"], 1)

            def split_product(target, pairs, start=True, stop=True):
                for i, ((a_hi, a_lo), (b_hi, b_lo)) in enumerate(pairs):
                    for k, (a, m) in enumerate(((a_hi, b_hi), (a_hi, b_lo), (a_lo, b_hi))):
                        last = nc.tensor.matmul(target, a, m, start=start and i == 0 and k == 0,
                                                stop=stop and i == len(pairs) - 1 and k == 2)
                return last

            pe.wait_ge(ident_ready, 1)
            pe.wait_ge(ffn_loaded, 16 * (2 + C))
            turn(None, 0, [a_raw[:, c * P:(c + 1) * P] for c in range(C)])
            turn(None, 1, [wr_raw[:, c * P:(c + 1) * P] for c in range(C)])
            turn(None, 2, [b_raw[:, o].rearrange("p h r -> p (h r)") for o in range(C)])

            with pe.Fori(0, NB) as b:
                base = ln_at("lo_done", b)
                for t in range(NT):
                    pe.wait_ge(sems["xn_ready"], ln_at("xn_ready", b) + t + 1)
                    turn(base, t, [x_normed[:, t, c * P:(c + 1) * P] for c in range(C)])

                def run(plan, at, start, g):
                    unit_of = units(plan)
                    base = start("lo_done")
                    ready = b * NG + g + 1
                    def turn_what(what, *which):
                        unit = unit_of[(what, *which)]
                        if what == "p":
                            s, j = which
                            if j == 0:
                                pe.wait_ge(sems["p_ready"], at("p_ready") + (s + 1) * G)
                            sources = [probs[:, s % 2, h, j * P:(j + 1) * P] for h in range(G)]
                        elif what == "q":
                            pe.wait_ge(sems["q_normed"], at("q_normed") + which[0])
                            sources = [qn[:, h, :] for h in range(G)]
                        elif what == "k":
                            if which[0] == 0:
                                pe.wait_ge(sems["k_normed"], start("k_normed") + 1)
                            sources = [k_norm[:, t, :] for t in range(4 * which[0], 4 * which[0] + 4)]
                        elif what == "wkv":
                            if which[0] == 0:
                                pe.wait_ge(wkv_loaded, 32 * ready)
                            sources = [wkv_raw[:, m, c * P:(c + 1) * P]
                                       for c in (2 * which[0], 2 * which[0] + 1) for m in range(2)]
                        elif what == "wq":
                            if which[0] == 0:
                                pe.wait_ge(wq_loaded, 16 * ready)
                            sources = [wq_raw[:, h, which[0] * P:(which[0] + 1) * P] for h in range(G)]
                        elif what == "wo":
                            if which[0] == 0:
                                pe.wait_ge(wo_loaded, 16 * (ready if plan is LAST_GROUP else ready - 1))
                            sources = [wo_raw[:, c, which[0] * P:(which[0] + 1) * P] for c in range(C)]
                        turn(base, unit, sources)

                    def q_part(s, c):
                        if c == 0:
                            if plan is PREPARE and s == NT:
                                pe.wait_ge(sems["lo_done"], base + unit_of["wq", C - 1] + 1)
                            elif plan is GROUP and s == NT:
                                pe.wait_ge(sems["lo_done"], base + unit_of["wq", C - 1] + 1)
                            if not (plan is PREPARE and s == NT):
                                pe.wait_ge(sems["q_normed"], at("q_normed") + s - 1)
                        tok = slice(s % NT * P, (s % NT + 1) * P)
                        last = split_product(q_ps[:], [((xnT_hi[:, c, tok], xnT_lo[:, c, tok]), (wqT_hi[:, c, :], wqT_lo[:, c, :]))],
                                             start=c == 0, stop=c == C - 1)
                        if c == C - 1:
                            last.then_inc(sems["q_full"], 1)

                    def scores(s, h):
                        L = (s + 1) * P
                        n = s * G + h
                        if h == 0 and s == 0:
                            pe.wait_ge(sems["lo_done"], base)
                        elif h == 0:
                            pe.wait_ge(sems["lo_done"], base + unit_of["q", s] + 1)
                        if L > 512:
                            pe.wait_ge(sems["s_max"], at("s_max") + n)
                        elif n >= 2:
                            pe.wait_ge(sems["s_max"], at("s_max") + n - 1)
                        for c in range(0, L, 512):
                            w = min(512, L - c)
                            at_col = 512 * (h % 2) if L <= 512 else c
                            last = split_product(s_ps[:, at_col:at_col + w],
                                                 [((qT_hi[:, s % 2, h, :], qT_lo[:, s % 2, h, :]),
                                                   (kT_hi[:, c:c + w], kT_lo[:, c:c + w]))])
                        last.then_inc(sems["s_full"], 1)

                    def kv(i):
                        if i == 0 and plan is PREPARE:
                            pe.wait_ge(sems["lo_done"], base + unit_of["wkv", C // 2 - 1] + 1)
                        elif i == 0:
                            pe.wait_ge(sems["s_max"], at("s_max") + NT * G)
                        if i >= 2:
                            pe.wait_ge(sems["kv_copied"], start("kv_copied") + i - 1)
                        for t in range(2):
                            tok = slice((2 * i + t) * P, (2 * i + t + 1) * P)
                            col = 512 * (i % 2) + t * 2 * HD
                            last = split_product(s_ps[:, col:col + 2 * HD],
                                                 [((xnT_hi[:, c, tok], xnT_lo[:, c, tok]), (wkvT_hi[:, c, :], wkvT_lo[:, c, :]))
                                                  for c in range(C)])
                        last.then_inc(sems["kv_full"], 1)

                    def values(s, j):
                        if s == 0:
                            pe.wait_ge(sems["v_lo_done"], at("v_lo_done"))
                        r = piece(s, j) % RING
                        pe.wait_ge(sems["lo_done"], base + unit_of["p", s, j] + 1)
                        last = split_product(o_ps[:], [((v_hi[:, j, :], v_lo[:, j, :]), (pT_hi[:, r, :], pT_lo[:, r, :]))],
                                             start=j == 0, stop=j == s)
                        if j == s:
                            last.then_inc(sems["o_full"], 1)

                    def y_product(s):
                        pe.wait_ge(sems["o_lo"], at("o_lo") + s + 1)
                        if s == 0:
                            pe.wait_ge(sems["lo_done"], base + unit_of["wo", G - 1] + 1)
                        else:
                            pe.wait_ge(sems["y_added"], at("y_added") + s)
                        split_product(y_ps[:], [((oT_hi[:, h, :], oT_lo[:, h, :]), (woT_hi[:, h, :], woT_lo[:, h, :]))
                                                for h in range(G)]).then_inc(sems["y_full"], 1)

                    follow({"turn": turn_what, "q_part": q_part, "scores": scores, "kv": kv, "values": values,
                            "y": y_product}, plan)

                run_plans(pe, run, b, True)

                def fat(name):
                    return ffn_at(name, b)

                for i in range(NT + 4):
                    if i < NT:
                        pe.wait_ge(sems["xn_ready"], fat("xn_ready") + i + 1)
                        turn(fat("lo_done"), UNIT_X[i], [x_normed[:, i, c * P:(c + 1) * P] for c in range(C)])
                    if 0 <= i - 1 < NT:
                        t = i - 1
                        pe.wait_ge(sems["lo_done"], fat("lo_done") + UNIT_X[t] + 1)
                        if t >= 2:
                            pe.wait_ge(sems["f_low"], fat("f_low") + t - 1)
                        for c in range(C):
                            last = nc.tensor.matmul((q_ps, o_ps)[t % 2][:, 0:P + NE], x_turned[:, t, c * P:(c + 1) * P],
                                                    arT[:, c, :], start=c == 0, stop=c == C - 1)
                        last.then_inc(sems["f_full"], 1)
                    if 0 <= i - 3 < NT:
                        t = i - 3
                        pe.wait_ge(sems["f_low"], fat("f_low") + t + 1)
                        turn(fat("lo_done"), UNIT_LOW[t], [low_gated[:, t, :]])
                    if 0 <= i - 4 < NT:
                        t = i - 4
                        pe.wait_ge(sems["lo_done"], fat("lo_done") + UNIT_LOW[t] + 1)
                        if t:
                            pe.wait_ge(sems["f_added"], fat("f_added") + t)
                        nc.tensor.matmul(y_ps[:], low_turned[:, t, :], bT[:], start=True, stop=True).then_inc(sems["f_out"], 1)


_INS = ["L0_attn_x", "L0_attn_Wq", "L0_attn_Wk", "L0_attn_Wv", "L0_attn_Wo", "L0_attn_q_norm_w", "L0_attn_k_norm_w",
        "L0_ffn_A", "L0_ffn_B", "L0_ffn_Wr", "L0_ffn_br"]


def kernel(**inputs):
    import concourse.bacc as bacc
    from concourse.bass_utils import run_bass_kernel_spmd

    nc = bacc.Bacc("TRN2", target_bir_lowering=False, num_devices=1)
    arrays, args = {}, []
    for name in _INS:
        a = np.ascontiguousarray(inputs[name])
        arrays[f"in_{name}"] = a
        args.append(nc.dram_tensor(f"in_{name}", a.shape, mybir.dt.from_np(a.dtype), kind="ExternalInput").ap())
    shape = inputs["L0_attn_x"].shape
    args.append(nc.dram_tensor("out_0", shape, F32, kind="ExternalOutput").ap())
    attention_lora_block(nc, *args)
    return run_bass_kernel_spmd(nc, [arrays], core_ids=[0]).results[0]["out_0"]
```

```python
import itertools
import math
from contextlib import ExitStack

import numpy as np

import concourse.bass as bass
from concourse import mybir

ALU = mybir.AluOpType
ACT = mybir.ActivationFunctionType
F32 = mybir.dt.float32
F32R = mybir.dt.float32r

P = 128
LN_EPS = 1e-5
RMS_EPS = 1e-6
NEG_INF = -1e30
LORA_SCALING = 32 / 16
BIG = 3e38

GROUP_PLAN = (
    "turn.wo.0 high.wo.0 low.wo.0 scores.0.0 max.0.0 turn.wo.1 high.wo.1 low.wo.1 scores.0.1 exp.0.0 max.0.1 "
    "normalise.0.0 scores.0.2 norm_q.1 turn.wo.2 high.wo.2 low.wo.2 exp.0.1 max.0.2 normalise.0.1 turn.wo.3 "
    "high.wo.3 low.wo.3 scores.0.3 turn.q.1 high.q.1 low.q.1 max.0.3 exp.0.2 q_part.2.0 exp.0.3 normalise.0.2 "
    "invert.0.0 q_part.2.1 q_part.2.2 q_part.2.3 invert.0.1 normalise.0.3 inv_q.2 "
    "scores.1.0 max.1.0 scores.1.1 square_q.2 exp.1.0 max.1.1 scores.1.2 norm_q.2 exp.1.1 max.1.2 turn.p.0.0 "
    "high.p.0.0 low.p.0.0 scores.1.3 invert.1.0 normalise.1.0 normalise.1.1 max.1.3 normalise.1.2 turn.q.2 "
    "high.q.2 low.q.2 exp.1.2 q_part.3.0 q_part.3.1 invert.1.1 normalise.1.3 inv_q.3 exp.1.3 values.0.0 "
    "q_part.3.2 "
    "scores.2.0 split_o.0 max.2.0 square_q.3 q_part.3.3 turn.p.1.0 high.p.1.0 low.p.1.0 exp.2.0 y.0 scores.2.1 "
    "scores.2.2 norm_q.3 max.2.1 max.2.2 normalise.2.0 turn.p.1.1 high.p.1.1 low.p.1.1 add_y.0 values.1.0 "
    "turn.q.3 high.q.3 low.q.3 q_part.4.0 scores.2.3 exp.2.1 invert.2.0 normalise.2.1 values.1.1 max.2.3 "
    "exp.2.2 exp.2.3 q_part.4.1 q_part.4.2 normalise.2.2 normalise.2.3 split_o.1 invert.2.1 q_part.4.3 "
    "square_q.4 "
    "scores.3.0 inv_q.4 max.3.0 y.1 normalise.3.0 add_y.1 turn.p.2.0 high.p.2.0 low.p.2.0 scores.3.1 exp.3.0 "
    "max.3.1 turn.p.2.1 high.p.2.1 low.p.2.1 turn.p.2.2 high.p.2.2 low.p.2.2 norm_q.4 scores.3.2 max.3.2 "
    "exp.3.1 scores.3.3 invert.3.0 max.3.3 exp.3.2 values.2.0 values.2.1 turn.q.4 high.q.4 low.q.4 q_part.5.0 "
    "normalise.3.1 values.2.2 exp.3.3 q_part.5.1 q_part.5.2 normalise.3.2 split_o.2 q_part.5.3 "
    "scores.4.0 invert.3.1 y.2 max.4.0 normalise.3.3 square_q.5 exp.4.0 add_y.2 turn.p.3.0 high.p.3.0 "
    "low.p.3.0 scores.4.1 max.4.1 turn.p.3.1 high.p.3.1 low.p.3.1 inv_q.5 normalise.4.0 turn.p.3.2 high.p.3.2 "
    "low.p.3.2 values.3.0 scores.4.2 exp.4.1 max.4.2 turn.p.3.3 high.p.3.3 low.p.3.3 invert.4.0 values.3.1 "
    "values.3.2 norm_q.5 normalise.4.1 normalise.4.2 exp.4.2 scores.4.3 max.4.3 turn.wkv.0 high.wkv.0 "
    "low.wkv.0 turn.q.5 high.q.5 low.q.5 normalise.4.3 exp.4.3 values.3.3 q_part.6.0 q_part.6.1 q_part.6.2 "
    "scores.5.0 q_part.6.3 invert.4.1 split_o.3 max.5.0 add_y.3 y.3 square_q.6 turn.p.4.0 high.p.4.0 low.p.4.0 "
    "inv_q.6 scores.5.1 exp.5.0 max.5.1 turn.p.4.1 high.p.4.1 low.p.4.1 turn.p.4.2 high.p.4.2 low.p.4.2 "
    "turn.wkv.1 high.wkv.1 low.wkv.1 values.4.0 scores.5.2 max.5.2 exp.5.1 values.4.1 exp.5.2 norm_q.6 "
    "values.4.2 turn.p.4.3 high.p.4.3 low.p.4.3 scores.5.3 q_part.7.0 invert.5.0 normalise.5.0 normalise.5.1 "
    "max.5.3 q_part.7.1 turn.p.4.4 high.p.4.4 low.p.4.4 turn.q.6 high.q.6 low.q.6 normalise.5.2 exp.5.3 "
    "values.4.3 invert.5.1 q_part.7.2 values.4.4 split_o.4 q_part.7.3 "
    "scores.6.0 turn.wq.0 high.wq.0 low.wq.0 max.6.0 add_y.4 y.4 turn.p.5.0 high.p.5.0 low.p.5.0 scores.6.1 "
    "exp.6.0 max.6.1 turn.p.5.1 high.p.5.1 low.p.5.1 turn.wq.1 high.wq.1 low.wq.1 turn.p.5.2 high.p.5.2 "
    "low.p.5.2 values.5.0 turn.wq.2 high.wq.2 low.wq.2 turn.p.5.3 high.p.5.3 low.p.5.3 normalise.5.3 "
    "scores.6.2 inv_q.7 normalise.6.0 square_q.7 max.6.2 exp.6.1 values.5.1 invert.6.0 turn.wq.3 high.wq.3 "
    "low.wq.3 normalise.6.1 norm_q.7 values.5.2 turn.p.5.4 high.p.5.4 low.p.5.4 scores.6.3 max.6.3 exp.6.2 "
    "turn.p.5.5 high.p.5.5 low.p.5.5 normalise.6.2 q_part.8.0 turn.q.7 high.q.7 low.q.7 exp.6.3 values.5.3 "
    "q_part.8.1 invert.6.1 q_part.8.2 normalise.6.3 split_o.5 values.5.4 values.5.5 "
    "scores.7.0 q_part.8.3 max.7.0 y.5 add_y.5 inv_q.8 turn.p.6.0 high.p.6.0 low.p.6.0 scores.7.1 max.7.1 "
    "turn.p.6.1 high.p.6.1 low.p.6.1 square_q.8 turn.p.6.2 high.p.6.2 low.p.6.2 values.6.0 normalise.7.0 "
    "turn.p.6.3 high.p.6.3 low.p.6.3 scores.7.2 max.7.2 exp.7.0 values.6.1 exp.7.1 norm_q.8 invert.7.0 "
    "normalise.7.1 values.6.2 turn.p.6.4 high.p.6.4 low.p.6.4 turn.p.6.5 high.p.6.5 low.p.6.5 scores.7.3 "
    "exp.7.2 max.7.3 values.6.3 turn.p.6.6 high.p.6.6 low.p.6.6 turn.q.8 high.q.8 low.q.8 values.6.4 "
    "invert.7.1 values.6.5 exp.7.3 split_o.6 values.6.6 "
    "kv.0 y.6 turn.p.7.0 high.p.7.0 low.p.7.0 turn.p.7.1 high.p.7.1 low.p.7.1 normalise.7.2 turn.p.7.2 "
    "high.p.7.2 low.p.7.2 kv.1 values.7.0 turn.p.7.3 high.p.7.3 low.p.7.3 values.7.1 turn.p.7.4 high.p.7.4 "
    "low.p.7.4 add_y.6 normalise.7.3 table.0 values.7.2 kv.2 turn.p.7.5 high.p.7.5 low.p.7.5 kv.3 values.7.3 "
    "inv_k turn.p.7.6 high.p.7.6 low.p.7.6 inv_q.9 values.7.4 turn.p.7.7 high.p.7.7 low.p.7.7 values.7.5 "
    "values.7.6 q_part.9.0 norm_k values.7.7 q_part.9.1 q_part.9.2 split_o.7 split_v turn.k.0 high.k.0 low.k.0 "
    "q_part.9.3 turn.k.1 high.k.1 low.k.1 table.1 table.2 y.7 square_q.9 add_y.7 table.3 "
)


def alibi_slopes(n_heads):
    start = 2 ** (-2 ** (-(math.log2(n_heads) - 3)))
    return np.array([start * start ** i for i in range(n_heads)], dtype=np.float32)


def attention_lora_block(nc, x, Wq, Wk, Wv, Wo, q_norm_w, k_norm_w, A, B, Wr, br, out):
    NB, S, DM = x.shape
    HD = q_norm_w.shape[0]
    H = Wq.shape[0] // HD
    NG = Wk.shape[0] // HD
    G = H // NG
    NE, RK, _ = A.shape
    NT = S // P
    C = DM // P
    W512 = G * HD
    assert HD == P and W512 == 512 and DM == 512 and NE * RK == P and S == 1024
    slopes = alibi_slopes(H)
    CARRIERS = 16
    RING = 3
    LAG = RING - 1

    def q_parts(s):
        return [("q_part", s, c) for c in range(C)] + [("square_q", s)]

    PREPARE = ([("turn", "wkv", i) for i in range(C // 2)] + [("turn", "wq", c) for c in range(C)]
               + [("table", 0)] + [("kv", i) for i in range(NT // 2)] + [("inv_k",)] + q_parts(NT) + [("inv_q", NT)]
               + [("norm_k",), ("turn", "k", 0), ("turn", "k", 1), ("split_v",), ("norm_q", NT), ("turn", "q", NT)]
               + q_parts(NT + 1) + [("inv_q", NT + 1)] + [("table", h) for h in range(1, G)])
    def in_parts(plan):
        parts = []
        for kind, *what in plan:
            parts.append((kind, *what))
            if kind == "turn":
                parts += [("high", *what), ("low", *what)]
            if kind == "scores":
                parts.append(("max", *what))
            if kind == "values" and what[0] == what[1]:
                parts.append(("split_o", what[0]))
            if kind == "y":
                parts.append(("add_y", what[0]))
        return parts

    PREPARE = in_parts(PREPARE)
    GROUP = [tuple(int(w) if w.isdigit() else w for w in item.split(".")) for item in GROUP_PLAN.split()]
    assert sorted(map(str, in_parts([x for x in GROUP if x[0] not in ("high", "low", "max", "split_o", "add_y")]))) == sorted(map(str, GROUP))

    def own(kind, *which):
        tile = kind in ("turn", "high", "low")
        return not (kind in ("kv", "inv_k", "norm_k", "split_v", "table") or tile and which[0] in ("wkv", "wq", "k")
                    or kind in ("q_part", "square_q", "inv_q", "norm_q") and which[0] >= NT
                    or tile and which[0] == "q" and which[1] >= NT)

    LAST_GROUP = [x for x in GROUP if own(*x)]

    UNIT_X, UNIT_LOW, n = {}, {}, 0
    for i in range(NT + 3):
        if i < NT:
            UNIT_X[i], n = n, n + 1
        if 0 <= i - 3 < NT:
            UNIT_LOW[i - 3], n = n, n + 1

    def signals(kind):
        return tuple(sum(x[0] == kind for x in plan) for plan in (PREPARE, GROUP, LAST_GROUP))

    q_counts = tuple(sum(x[0] == "q_part" and x[2] == C - 1 for x in plan) for plan in (PREPARE, GROUP, LAST_GROUP))
    COUNTS = {
        "turned": (3, NT, *signals("turn"), 2 * NT),
        "hi_done": (0, NT, *signals("turn"), 0),
        "lo_done": (3, NT, *signals("turn"), 2 * NT),
        "ln_stats": (0, NT, 0, 0, 0, NT), "ln_moments": (0, NT, 0, 0, 0, NT), "ln_var_eps": (0, 2, 0, 0, 0, 2),
        "ln_rstd": (0, 2, 0, 0, 0, 2), "xn_ready": (0, NT, 0, 0, 0, NT),
        "bias_ready": (0, 0, *signals("table"), 0),
        "kv_full": (0, 0, *signals("kv"), 0), "kv_squares": (0, 0, *signals("kv"), 0),
        "kv_copied": (0, 0, *signals("kv"), 0),
        "k_sum_eps": (0, 0, *signals("inv_k"), 0), "k_inv": (0, 0, *signals("inv_k"), 0),
        "k_normed": (0, 0, *signals("norm_k"), 0),
        "v_hi_done": (0, 0, *signals("split_v"), 0), "v_lo_done": (0, 0, *signals("split_v"), 0),
        "q_full": (0, 0, *q_counts, 0), "q_squares": (0, 0, *q_counts, 0), "q_sum_eps": (0, 0, *q_counts, 0),
        "q_inv": (0, 0, *q_counts, 0), "q_normed": (0, 0, *signals("norm_q"), 0),
        "s_full": (0, 0, *signals("scores"), 0), "s_max": (0, 0, *signals("scores"), 0),
        "p_exp": (0, 0, *signals("exp"), 0), "p_inv": (0, 0, *signals("invert"), 0),
        "p_ready": (0, 0, *signals("normalise"), 0),
        "o_full": (0, 0, *signals("y"), 0), "o_hi": (0, 0, *signals("y"), 0), "o_lo": (0, 0, *signals("y"), 0),
        "y_full": (0, 0, *signals("y"), 0), "y_added": (0, 0, *signals("y"), 0),
        "f_full": (0, 0, 0, 0, 0, NT), "f_max": (0, 0, 0, 0, 0, NT), "f_exp": (0, 0, 0, 0, 0, NT),
        "f_inv": (0, 0, 0, 0, 0, NT), "f_gate": (0, 0, 0, 0, 0, NT), "f_low": (0, 0, 0, 0, 0, NT),
        "f_out": (0, 0, 0, 0, 0, NT), "f_added": (0, 0, 0, 0, 0, NT),
    }

    def batch_at(name, b):
        pro, ln, prep, grp, last, ffn = COUNTS[name]
        return b * (ln + prep + (NG - 1) * grp + last + ffn) + pro

    def ln_at(name, b):
        return batch_at(name, b)

    def prepare_at(name, b):
        return batch_at(name, b) + COUNTS[name][1]

    def group_at(name, b, g):
        pro, ln, prep, grp, last, ffn = COUNTS[name]
        return batch_at(name, b) + g * grp + (ln + prep)

    def ffn_at(name, b):
        pro, ln, prep, grp, last, ffn = COUNTS[name]
        return batch_at(name, b) + (ln + prep + (NG - 1) * grp + last)

    def units(plan):
        return {x[1:]: n for n, x in enumerate(x for x in plan if x[0] == "turn")}

    def piece(s, j):
        return s * (s + 1) // 2 + j

    def follow(work, plan):
        for kind, *what in plan:
            if kind in work:
                work[kind](*what)

    with ExitStack() as ctx:
        def sb(name, shape, dt=F32):
            return ctx.enter_context(nc.sbuf_tensor(name, shape, dt))

        def psum(name, shape):
            return ctx.enter_context(nc.psum_tensor(name, shape, F32))

        def sem(name):
            return ctx.enter_context(nc.semaphore(name))

        xnT_hi = sb("xnT_hi", [P, C, S], F32R)
        xnT_lo = sb("xnT_lo", [P, C, S], F32R)
        y = sb("y", [P, NT, DM])
        wqT_hi = sb("wqT_hi", [P, C, W512], F32R)
        wqT_lo = sb("wqT_lo", [P, C, W512], F32R)
        wkvT_hi = sb("wkvT_hi", [P, C, 2 * HD], F32R)
        wkvT_lo = sb("wkvT_lo", [P, C, 2 * HD], F32R)
        woT_hi = sb("woT_hi", [P, G, DM], F32R)
        woT_lo = sb("woT_lo", [P, G, DM], F32R)
        wq_raw = sb("wq_raw", [P, G, DM])
        wkv_raw = sb("wkv_raw", [P, 2, DM])
        wo_raw = sb("wo_raw", [P, C, W512])
        kT_hi = sb("kT_hi", [P, S], F32R)
        kT_lo = sb("kT_lo", [P, S], F32R)
        v_hi = sb("v_hi", [P, NT, HD], F32R)
        v_lo = sb("v_lo", [P, NT, HD], F32R)
        rel = sb("rel", [P, S])
        bias = sb("bias", [P, G, S])
        probs = sb("probs", [P, 2, G, S])
        qn = sb("qn", [P, G, HD])
        qT_hi = sb("qT_hi", [P, 2, G, P], F32R)
        qT_lo = sb("qT_lo", [P, 2, G, P], F32R)
        pT_hi = sb("pT_hi", [P, RING, G * P], F32R)
        pT_lo = sb("pT_lo", [P, RING, G * P], F32R)
        oT_hi = sb("oT_hi", [P, G, P], F32R)
        oT_lo = sb("oT_lo", [P, G, P], F32R)
        arT = sb("arT", [P, C, P + NE])
        bT = sb("bT", [P, DM])
        ident = sb("ident", [P, P])
        slope_row = sb("slope_row", [P, H])
        minus_half = sb("minus_half", [P, NT])
        ln_eps = sb("ln_eps", [P, NT // 2])
        rms_eps = sb("rms_eps", [P, NT])
        scratch = sb("scratch", [P, CARRIERS, 1])
        wq_norm = sb("wq_norm", [P, 1])
        wk_norm = sb("wk_norm", [P, 1])
        wk_scaled = sb("wk_scaled", [P, 1])
        br_row = sb("br_row", [P, NE])
        stats = sb("stats", [P, NT, 6])
        moments = sb("moments", [P, NT, 2])
        var_eps = sb("var_eps", [P, NT])
        rstd = sb("rstd", [P, NT])
        k_sum = sb("k_sum", [P, NT])
        k_sum_eps_t = sb("k_sum_eps_t", [P, NT])
        k_inv_t = sb("k_inv_t", [P, NT])
        q_sum = sb("q_sum", [P, G])
        q_sum_eps_t = sb("q_sum_eps_t", [P, G])
        q_inv_t = sb("q_inv_t", [P, G])
        neg_max = sb("neg_max", [P, 2, G])
        p_sum = sb("p_sum", [P, 2, G])
        p_inv_t = sb("p_inv_t", [P, 2, G])
        f_neg_max = sb("f_neg_max", [P, NT])
        f_sum = sb("f_sum", [P, NT])
        f_inv_t = sb("f_inv_t", [P, NT])

        slots = probs[:].rearrange("p a h s -> p (a h) s")
        kv_raw = probs[:, 0, 0:2, :].rearrange("p a (t d) -> p (a t) d", d=2 * HD)
        k_norm = probs[:, 0, 2, :].rearrange("p (t d) -> p t d", d=HD)
        x_normed = slots[:, :, 0:DM]
        x_turned = slots[:, :, DM:2 * DM]
        low_gated = bias[:, 0, :].rearrange("p (t n) -> p t n", n=P)
        low_turned = bias[:, 1, :].rearrange("p (t n) -> p t n", n=P)
        a_raw = bias[:, 0, 0:DM]
        wr_raw = bias[0:NE, 1, 0:DM]
        b_raw = bias[:, 2, 0:DM].rearrange("p (h o r) -> p h o r", o=C, r=RK)
        b_sorted = bias[:, 3, 0:DM].rearrange("p (o h r) -> p o h r", o=C, r=RK)
        f_logits, f_weights, f_gates = (
            bias[:, 2, i * NT * NE:(i + 1) * NT * NE].rearrange("p (t n) -> p t n", n=NE) for i in range(3))

        s_ps = psum("s_ps", [P, 1024])
        turn_ps = [psum(f"turn_ps{i}", [P, 512]) for i in range(RING)]
        q_ps = psum("q_ps", [P, 512])
        o_ps = psum("o_ps", [P, 512])
        y_ps = psum("y_ps", [P, 512])

        sems = {name: sem(name) for name in COUNTS}
        ident_ready = sem("ident_ready")
        rel_ready = sem("rel_ready")
        tables_ready = sem("tables_ready")
        wk_scaled_ready = sem("wk_scaled_ready")
        pool_step = sem("pool_step")
        small_loaded = sem("small_loaded")
        ffn_loaded = sem("ffn_loaded")
        b_sorted_ready = sem("b_sorted_ready")
        x_loaded = [sem(f"x_loaded{i}") for i in range(NT)]
        wkv_loaded = sem("wkv_loaded")
        wq_loaded = sem("wq_loaded")
        wo_loaded = sem("wo_loaded")
        stored = [sem("stored_even"), sem("stored_odd")]

        block = ctx.enter_context(nc.Block())

        def run_plans(engine, run, b, with_group=False):
            def prepared(name):
                return prepare_at(name, b) + (COUNTS[name][2] - COUNTS[name][3])

            run(PREPARE, prepared, lambda name: prepare_at(name, b), *([0] if with_group else []))
            with engine.Fori(0, NG - 1) as g:
                run(GROUP, lambda name: group_at(name, b, g), lambda name: group_at(name, b, g),
                    *([g + 1] if with_group else []))
            run(LAST_GROUP, lambda name: group_at(name, b, NG - 1), lambda name: group_at(name, b, NG - 1),
                *([NG - 1] if with_group else []))

        @block.sync
        def _(sp):
            x_v = x.rearrange("b (t p) d -> b p t d", p=P)
            out_v = out.rearrange("b (t p) d -> b p t d", p=P)
            wq_v = Wq.rearrange("(g h p) d -> g p h d", h=G, p=P)
            wk_v = Wk.rearrange("(g p) d -> g p d", p=P)
            wv_v = Wv.rearrange("(g p) d -> g p d", p=P)
            wo_v = Wo.rearrange("(c p) (g n) -> g p c n", p=P, n=W512)

            def load_wqkv(g):
                sp.dma_start(wkv_raw[:, 0, :], wk_v[g]).then_inc(wkv_loaded, 16)
                sp.dma_start(wkv_raw[:, 1, :], wv_v[g]).then_inc(wkv_loaded, 16)
                sp.dma_start(wq_raw[:], wq_v[g]).then_inc(wq_loaded, 16)

            def load_wo(g):
                sp.dma_start(wo_raw[:], wo_v[g]).then_inc(wo_loaded, 16)

            wo_turned = units(GROUP)["wo", G - 1] + 1

            def load_next(b, g, following):
                sp.wait_ge(sems["turned"], group_at("turned", b, g))
                load_wqkv(following)
                sp.wait_ge(sems["turned"], group_at("turned", b, g) + wo_turned)
                load_wo(following)

            def load_x(b, t):
                sp.dma_start(y[:, t, :], x_v[b, :, t, :]).then_inc(x_loaded[t], 16)

            for t in range(NT):
                load_x(0, t)
            load_wqkv(0)
            load_wo(0)
            for b in range(NB):
                with sp.Fori(0, NG - 1) as g:
                    load_next(b, g, g + 1)
                if b < NB - 1:
                    load_next(b, NG - 1, 0)
                for t in range(NT + 1):
                    if t < NT:
                        sp.wait_ge(sems["f_added"], ffn_at("f_added", b) + t + 1)
                        sp.dma_start(out_v[b, :, t, :], y[:, t, :]).then_inc(stored[t % 2], 16)
                    if t:
                        sp.wait_ge(stored[(t - 1) % 2], 16 * (NT // 2 * b + (t - 1) // 2 + 1))
                        if b < NB - 1:
                            load_x(b + 1, t - 1)

        @block.scalar
        def _(act):
            act.dma_start(wk_norm[:], k_norm_w.rearrange("(p a) -> p a", a=1)).then_inc(small_loaded, 16)
            act.dma_start(wq_norm[:], q_norm_w.rearrange("(p a) -> p a", a=1)).then_inc(small_loaded, 16)
            act.dma_start(br_row[:], br.rearrange("(a n) -> a n", a=1).broadcast_to((P, NE))).then_inc(small_loaded, 16)
            act.dma_start(a_raw, A.rearrange("h r d -> (h r) d")).then_inc(ffn_loaded, 16)
            act.dma_start(wr_raw, Wr).then_inc(ffn_loaded, 16)
            act.dma_start(b_raw, B.rearrange("h (p o) r -> p h o r", o=C)).then_inc(ffn_loaded, 16)
            act.wait_ge(ffn_loaded, 48)
            nc.scalar.activation(b_sorted.rearrange("p o h r -> p h o r"), b_raw, ACT.Copy).then_inc(b_sorted_ready, 1)
            act.wait_ge(sems["turned"], 1)
            nc.scalar.activation(arT[:, :, 0:P], turn_ps[0][:].rearrange("p (c n) -> p c n", c=C),
                                 ACT.Copy).then_inc(sems["lo_done"], 1)
            act.wait_ge(sems["turned"], 2)
            nc.scalar.activation(arT[:, :, P:P + NE], turn_ps[1][:, 0:C * NE].rearrange("p (c n) -> p c n", c=C),
                                 ACT.Copy).then_inc(sems["lo_done"], 1)
            act.wait_ge(sems["turned"], 3)
            nc.scalar.activation(bT[:].rearrange("p (n o) -> p o n", o=C), turn_ps[2][:].rearrange("p (o n) -> p o n", o=C),
                                 ACT.Copy).then_inc(sems["lo_done"], 1)
            act.wait_ge(small_loaded, 48)
            act.wait_ge(wk_scaled_ready, 1)

            def high(base, unit, target, source, scale=None):
                act.wait_ge(sems["turned"], base + unit + 1)
                if scale is None:
                    nc.scalar.activation(target, source, ACT.Copy).then_inc(sems["hi_done"], 1)
                else:
                    nc.scalar.activation(target, source, ACT.Copy, scale=scale).then_inc(sems["hi_done"], 1)

            with act.Fori(0, NB) as b:
                base = ln_at("turned", b)
                for t in range(NT):
                    high(base, t, xnT_hi[:, :, t * P:(t + 1) * P],
                         turn_ps[t % RING][:].rearrange("p (c n) -> p c n", c=C))

                def run(plan, at, start):
                    unit_of = units(plan)
                    base = start("turned")

                    def turn(what, *which):
                        unit = unit_of[(what, *which)]
                        bank = turn_ps[unit % RING][:]
                        if what == "p":
                            high(base, unit, pT_hi[:, piece(*which) % RING, :], bank)
                        elif what == "q":
                            high(base, unit, qT_hi[:, which[0] % 2].rearrange("p h n -> p (h n)"), bank, wq_norm[:])
                        elif what == "k":
                            high(base, unit, kT_hi[:, which[0] * 512:(which[0] + 1) * 512], bank, wk_scaled[:])
                        elif what == "wkv":
                            i = which[0]
                            high(base, unit, wkvT_hi[:, 2 * i:2 * i + 2, :].rearrange("p c n -> p (c n)"), bank)
                        elif what == "wq":
                            high(base, unit, wqT_hi[:, which[0], :], bank)
                        elif what == "wo":
                            high(base, unit, woT_hi[:, which[0], :], bank)

                    def exp(s, h):
                        n = s * G + h
                        L = (s + 1) * P
                        act.wait_ge(sems["s_max"], at("s_max") + n + 1)
                        row = probs[:, s % 2, h, 0:L]
                        nc.scalar.activation(row, row, ACT.Exp, bias=neg_max[:, s % 2, h:h + 1], scale=-1.0,
                                             accum_out=p_sum[:, s % 2, h:h + 1]).then_inc(sems["p_exp"], 1)

                    def square_q(s):
                        act.wait_ge(sems["q_full"], at("q_full") + s - 1)
                        for h in range(G):
                            last = nc.scalar.activation(qn[:, h, :], q_ps[:, h * HD:(h + 1) * HD], ACT.Square,
                                                        accum_out=q_sum[:, h:h + 1])
                        last.then_inc(sems["q_squares"], 1)

                    def kv(i):
                        act.wait_ge(sems["kv_full"], start("kv_full") + i + 1)
                        for t in range(2):
                            last = nc.scalar.activation(k_norm[:, 2 * i + t, :], s_ps[:, 512 * (i % 2) + t * 2 * HD:][:, 0:HD],
                                                        ACT.Square, accum_out=k_sum[:, 2 * i + t:2 * i + t + 1])
                        last.then_inc(sems["kv_squares"], 1)

                    def split_v():
                        act.wait_ge(sems["kv_copied"], start("kv_copied") + NT // 2)
                        if plan is GROUP:
                            act.wait_ge(sems["o_full"], at("o_full") + NT)
                        nc.scalar.activation(v_hi[:], kv_raw[:, :, HD:2 * HD], ACT.Copy).then_inc(sems["v_hi_done"], 1)

                    def split_o(s):
                        act.wait_ge(sems["o_full"], at("o_full") + s + 1)
                        nc.scalar.activation(oT_hi[:].rearrange("p h n -> p (h n)"), o_ps[:],
                                             ACT.Copy).then_inc(sems["o_hi"], 1)

                    follow({"high": turn, "exp": exp, "square_q": square_q, "kv": kv, "split_v": split_v,
                            "split_o": split_o}, plan)

                run_plans(act, run, b)
                for t in range(NT):
                    act.wait_ge(sems["f_max"], ffn_at("f_max", b) + t + 1)
                    nc.scalar.activation(f_weights[:, t, :], f_logits[:, t, :], ACT.Exp, bias=f_neg_max[:, t:t + 1],
                                         scale=-1.0, accum_out=f_sum[:, t:t + 1]).then_inc(sems["f_exp"], 1)

        @block.gpsimd
        def _(pool):
            nc.gpsimd.memset(ident[:], 0.0).then_inc(pool_step, 1)
            nc.gpsimd.iota(rel[:], [[1, S]], base=-(S - P), channel_multiplier=-1,
                           allow_small_or_imprecise_dtypes=True).then_inc(pool_step, 1)
            pool.wait_ge(pool_step, 2)
            nc.gpsimd.affine_select(out=ident[:], in_=ident[:], compare_op=ALU.not_equal, fill=1.0, base=0,
                                    pattern=[[-1, P]], channel_multiplier=1).then_inc(ident_ready, 1)
            nc.gpsimd.affine_select(out=rel[:], in_=rel[:], compare_op=ALU.is_ge, fill=NEG_INF, base=S - P,
                                    pattern=[[-1, S]], channel_multiplier=1).then_inc(rel_ready, 1)
            pool.wait_ge(rel_ready, 1)
            pool.wait_ge(tables_ready, 1)

            def inverse_root(base_eps, target, eps_t, source, eps, n, name_eps, name_out):
                nc.gpsimd.tensor_tensor(eps_t, source, eps, ALU.add).then_inc(sems[name_eps], 1)
                pool.wait_ge(sems[name_eps], base_eps + 1)
                nc.gpsimd.tensor_tensor(target, eps_t, minus_half[:, 0:n], ALU.pow).then_inc(sems[name_out], 1)

            def layer_norm(at):
                half = NT // 2
                for i in range(2):
                    r = slice(i * half, (i + 1) * half)
                    pool.wait_ge(sems["ln_moments"], at("ln_moments") + half * (i + 1))
                    inverse_root(at("ln_var_eps") + i, rstd[:, r], var_eps[:, r], moments[:, r, 1], ln_eps[:], half,
                                 "ln_var_eps", "ln_rstd")

            with pool.Fori(0, NB) as b:
                layer_norm(lambda name: ln_at(name, b))

                def run(plan, at, start, g):
                    def inv_q(s):
                        n = at("q_sum_eps") + s - 2
                        pool.wait_ge(sems["q_squares"], at("q_squares") + s - 1)
                        inverse_root(n, q_inv_t[:], q_sum_eps_t[:], q_sum[:], rms_eps[:, 0:G], G, "q_sum_eps", "q_inv")

                    def inv_k():
                        pool.wait_ge(sems["kv_squares"], start("kv_squares") + NT // 2)
                        inverse_root(start("k_sum_eps"), k_inv_t[:], k_sum_eps_t[:], k_sum[:], rms_eps[:], NT,
                                     "k_sum_eps", "k_inv")

                    def normalise(s, h):
                        L = (s + 1) * P
                        if h % 2 == 0:
                            pool.wait_ge(sems["p_inv"], at("p_inv") + 2 * s + h // 2 + 1)
                        row = probs[:, s % 2, h, 0:L]
                        nc.gpsimd.tensor_tensor(row, row, p_inv_t[:, s % 2, h:h + 1].to_broadcast((P, L)),
                                                ALU.mult).then_inc(sems["p_ready"], 1)

                    def table(h):
                        if h == 0:
                            pool.wait_ge(sems["turned"], start("turned") + 1)
                        if plan is GROUP:
                            pool.wait_ge(sems["s_max"], at("s_max") + (NT - 1) * G + h + 1)
                        nc.gpsimd.tensor_tensor(bias[:, h, :], rel[:],
                                                slope_row[:, bass.ds(g * G + h, 1)].to_broadcast((P, S)),
                                                ALU.mult).then_inc(sems["bias_ready"], 1)

                    follow({"inv_q": inv_q, "inv_k": inv_k, "normalise": normalise, "table": table}, plan)

                run_plans(pool, run, b, True)
                layer_norm(lambda name: ffn_at(name, b))

        @block.vector
        def _(dve):
            nc.vector.memset(minus_half[:], -0.5)
            nc.vector.memset(ln_eps[:], LN_EPS)
            nc.vector.memset(rms_eps[:], HD * RMS_EPS)
            for h in range(H):
                last = nc.vector.memset(slope_row[:, h:h + 1], float(slopes[h]))
            last.then_inc(tables_ready, 1)
            dve.wait_ge(small_loaded, 48)

            carriers = itertools.count()

            def alone():
                nc.vector.memset(scratch[:, next(carriers) % CARRIERS, :], 0.0)

            nc.vector.tensor_scalar(wk_scaled[:], wk_norm[:], math.sqrt(HD), None, ALU.mult).then_inc(wk_scaled_ready, 1)
            dve.wait_ge(wk_scaled_ready, 1)

            def layer_norm(at, ready):
                half = NT // 2

                def statistics(tiles):
                    for t in tiles:
                        ready(t)
                        nc.vector.bn_stats(stats[:, t, :], y[:, t, :]).then_inc(sems["ln_stats"], 1)

                def mean_variance(tiles):
                    for t in tiles:
                        dve.wait_ge(sems["ln_stats"], at("ln_stats") + t + 1)
                        alone()
                        nc.vector.bn_aggr(moments[:, t, :], stats[:, t, :]).then_inc(sems["ln_moments"], 1)

                def normalise(tiles):
                    dve.wait_ge(sems["ln_rstd"], at("ln_rstd") + tiles[0] // half + 1)
                    for t in tiles:
                        nc.vector.tensor_scalar(x_normed[:, t, :], y[:, t, :], moments[:, t, 0:1], rstd[:, t:t + 1],
                                                ALU.subtract, ALU.mult).then_inc(sems["xn_ready"], 1)

                first, second = range(half), range(half, NT)
                statistics(first)
                mean_variance(first)
                statistics(second)
                normalise(first)
                mean_variance(second)
                normalise(second)

            def low(base, unit, target, source, high, scale=None):
                dve.wait_ge(sems["hi_done"], base + unit + 1)
                if scale is None:
                    nc.vector.tensor_tensor(target, source, high.bitcast(F32), ALU.subtract).then_inc(sems["lo_done"], 1)
                else:
                    nc.vector.scalar_tensor_tensor(target, source, scale, high.bitcast(F32), ALU.mult,
                                                   ALU.subtract).then_inc(sems["lo_done"], 1)

            with dve.Fori(0, NB) as b:
                def x_ready(t):
                    dve.wait_ge(x_loaded[t], b * 16 + 16)

                layer_norm(lambda name: ln_at(name, b), x_ready)
                base = ln_at("hi_done", b)
                for t in range(NT):
                    cols = slice(t * P, (t + 1) * P)
                    low(base, t, xnT_lo[:, :, cols], turn_ps[t % RING][:].rearrange("p (c n) -> p c n", c=C),
                        xnT_hi[:, :, cols])

                def run(plan, at, start):
                    unit_of = units(plan)
                    base = start("hi_done")

                    def turn(what, *which):
                        unit = unit_of[(what, *which)]
                        bank = turn_ps[unit % RING][:]
                        if what == "p":
                            r = piece(*which) % RING
                            low(base, unit, pT_lo[:, r, :], bank, pT_hi[:, r, :])
                        elif what == "q":
                            flat = "p h n -> p (h n)"
                            low(base, unit, qT_lo[:, which[0] % 2].rearrange(flat), bank, qT_hi[:, which[0] % 2].rearrange(flat),
                                wq_norm[:])
                        elif what == "k":
                            cols = slice(which[0] * 512, (which[0] + 1) * 512)
                            low(base, unit, kT_lo[:, cols], bank, kT_hi[:, cols], wk_scaled[:])
                        elif what == "wkv":
                            chunks = slice(2 * which[0], 2 * which[0] + 2)
                            low(base, unit, wkvT_lo[:, chunks, :].rearrange("p c n -> p (c n)"), bank,
                                wkvT_hi[:, chunks, :].rearrange("p c n -> p (c n)"))
                        elif what == "wq":
                            low(base, unit, wqT_lo[:, which[0], :], bank, wqT_hi[:, which[0], :])
                        elif what == "wo":
                            low(base, unit, woT_lo[:, which[0], :], bank, woT_hi[:, which[0], :])

                    def score_max(s, h):
                        n = s * G + h
                        L = (s + 1) * P
                        if s == 0:
                            dve.wait_ge(sems["bias_ready"], at("bias_ready") - G + h + 1)
                        dve.wait_ge(sems["s_full"], at("s_full") + n + 1)
                        alone()
                        at_col = 512 * (h % 2) if L <= 512 else 0
                        nc.vector.tensor_tensor_reduce(
                            out=probs[:, s % 2, h, 0:L], in0=s_ps[:, at_col:at_col + L], in1=bias[:, h, S - L:S],
                            scale=-1.0, scalar=BIG, op0=ALU.add, op1=ALU.min,
                            accum_out=neg_max[:, s % 2, h:h + 1]).then_inc(sems["s_max"], 1)

                    def invert(s, i):
                        n = s * G + 2 * i + 1
                        dve.wait_ge(sems["p_exp"], at("p_exp") + n + 1)
                        nc.vector.reciprocal(p_inv_t[:, s % 2, 2 * i:2 * i + 2],
                                             p_sum[:, s % 2, 2 * i:2 * i + 2]).then_inc(sems["p_inv"], 1)

                    def norm_q(s):
                        dve.wait_ge(sems["q_inv"], at("q_inv") + s - 1)
                        nc.vector.tensor_tensor(qn[:], q_ps[:].rearrange("p (h d) -> p h d", h=G),
                                                q_inv_t[:].unsqueeze(2).to_broadcast((P, G, HD)),
                                                ALU.mult).then_inc(sems["q_normed"], 1)

                    def kv(i):
                        dve.wait_ge(sems["kv_squares"], start("kv_squares") + i + 1)
                        nc.vector.tensor_copy(kv_raw[:, 2 * i:2 * i + 2, :],
                                              s_ps[:, 512 * (i % 2):512 * (i % 2 + 1)].rearrange("p (t n) -> p t n", t=2))\
                            .then_inc(sems["kv_copied"], 1)

                    def norm_k():
                        dve.wait_ge(sems["kv_copied"], start("kv_copied") + NT // 2)
                        dve.wait_ge(sems["k_inv"], start("k_inv") + 1)
                        nc.vector.tensor_tensor(k_norm[:], kv_raw[:, :, 0:HD],
                                                k_inv_t[:].unsqueeze(2).to_broadcast((P, NT, HD)),
                                                ALU.mult).then_inc(sems["k_normed"], 1)

                    def split_v():
                        dve.wait_ge(sems["v_hi_done"], start("v_hi_done") + 1)
                        nc.vector.tensor_tensor(v_lo[:], kv_raw[:, :, HD:2 * HD], v_hi[:].bitcast(F32),
                                                ALU.subtract).then_inc(sems["v_lo_done"], 1)

                    def split_o(s):
                        dve.wait_ge(sems["o_hi"], at("o_hi") + s + 1)
                        nc.vector.tensor_tensor(oT_lo[:].rearrange("p h n -> p (h n)"), o_ps[:],
                                                oT_hi[:].rearrange("p h n -> p (h n)").bitcast(F32),
                                                ALU.subtract).then_inc(sems["o_lo"], 1)

                    def add_y(s):
                        dve.wait_ge(sems["y_full"], at("y_full") + s + 1)
                        nc.vector.tensor_tensor(y[:, s, :], y_ps[:], y[:, s, :], ALU.add).then_inc(sems["y_added"], 1)

                    follow({"low": turn, "max": score_max, "invert": invert, "norm_q": norm_q, "kv": kv, "norm_k": norm_k,
                            "split_v": split_v, "split_o": split_o, "add_y": add_y}, plan)

                run_plans(dve, run, b)

                def fat(name):
                    return ffn_at(name, b)

                def y_ready(t):
                    if t == 0:
                        dve.wait_ge(sems["y_added"], fat("y_added"))

                layer_norm(fat, y_ready)
                for i in range(NT + 4):
                    if i < NT:
                        dve.wait_ge(sems["turned"], fat("turned") + UNIT_X[i] + 1)
                        nc.vector.tensor_copy(x_turned[:, i, :], turn_ps[UNIT_X[i] % RING][:]).then_inc(sems["lo_done"], 1)
                    if 0 <= i - 1 < NT:
                        t = i - 1
                        dve.wait_ge(sems["f_full"], fat("f_full") + t + 1)
                        alone()
                        nc.vector.tensor_tensor_reduce(
                            out=f_logits[:, t, :], in0=(q_ps, o_ps)[t % 2][:, P:P + NE], in1=br_row[:], scale=-1.0,
                            scalar=BIG, op0=ALU.add, op1=ALU.min, accum_out=f_neg_max[:, t:t + 1]).then_inc(sems["f_max"], 1)
                    if 0 <= i - 2 < NT:
                        t = i - 2
                        dve.wait_ge(sems["f_exp"], fat("f_exp") + t + 1)
                        nc.vector.reciprocal(f_inv_t[:, t:t + 1], f_sum[:, t:t + 1]).then_inc(sems["f_inv"], 1)
                        dve.wait_ge(sems["f_inv"], fat("f_inv") + t + 1)
                        nc.vector.tensor_scalar(f_gates[:, t, :], f_weights[:, t, :], f_inv_t[:, t:t + 1],
                                                NE * LORA_SCALING, ALU.mult, ALU.mult).then_inc(sems["f_gate"], 1)
                        dve.wait_ge(sems["f_gate"], fat("f_gate") + t + 1)
                        nc.vector.tensor_tensor(low_gated[:, t, :].rearrange("p (h r) -> p h r", r=RK),
                                                (q_ps, o_ps)[t % 2][:, 0:P].rearrange("p (h r) -> p h r", r=RK),
                                                f_gates[:, t, :].unsqueeze(2).to_broadcast((P, NE, RK)),
                                                ALU.mult).then_inc(sems["f_low"], 1)
                    if 0 <= i - 3 < NT:
                        t = i - 3
                        dve.wait_ge(sems["turned"], fat("turned") + UNIT_LOW[t] + 1)
                        nc.vector.tensor_copy(low_turned[:, t, :], turn_ps[UNIT_LOW[t] % RING][:, 0:P]).then_inc(sems["lo_done"], 1)
                    if 0 <= i - 4 < NT:
                        t = i - 4
                        dve.wait_ge(sems["f_out"], fat("f_out") + t + 1)
                        nc.vector.tensor_tensor(y[:, t, :], y_ps[:], y[:, t, :], ALU.add).then_inc(sems["f_added"], 1)

        @block.tensor
        def _(pe):
            def turn(base, unit, sources, start_free=None):
                if base is not None:
                    pe.wait_ge(sems["lo_done"], base + max(0, unit - RING + 1))
                width, rows = sources[0].shape[0], sources[0].shape[1]
                for i, source in enumerate(sources):
                    last = nc.tensor.transpose(turn_ps[unit % RING][0:rows, i * width:(i + 1) * width],
                                               source, ident[0:width, 0:width])
                last.then_inc(sems["turned"], 1)

            def split_product(target, pairs, start=True, stop=True):
                for i, ((a_hi, a_lo), (b_hi, b_lo)) in enumerate(pairs):
                    for k, (a, m) in enumerate(((a_hi, b_hi), (a_hi, b_lo), (a_lo, b_hi))):
                        last = nc.tensor.matmul(target, a, m, start=start and i == 0 and k == 0,
                                                stop=stop and i == len(pairs) - 1 and k == 2)
                return last

            pe.wait_ge(ident_ready, 1)
            pe.wait_ge(ffn_loaded, 48)
            turn(None, 0, [a_raw[:, c * P:(c + 1) * P] for c in range(C)])
            turn(None, 1, [wr_raw[:, c * P:(c + 1) * P] for c in range(C)])
            pe.wait_ge(b_sorted_ready, 1)
            turn(None, 2, [b_sorted[:, o].rearrange("p h r -> p (h r)") for o in range(C)])

            with pe.Fori(0, NB) as b:
                base = ln_at("lo_done", b)
                for t in range(NT):
                    pe.wait_ge(sems["xn_ready"], ln_at("xn_ready", b) + t + 1)
                    turn(base, t, [x_normed[:, t, c * P:(c + 1) * P] for c in range(C)])

                def run(plan, at, start, g):
                    unit_of = units(plan)
                    base = start("lo_done")
                    ready = b * NG + g + 1
                    def turn_what(what, *which):
                        unit = unit_of[(what, *which)]
                        if what == "p":
                            s, j = which
                            if j == 0:
                                pe.wait_ge(sems["p_ready"], at("p_ready") + (s + 1) * G)
                            sources = [probs[:, s % 2, h, j * P:(j + 1) * P] for h in range(G)]
                        elif what == "q":
                            pe.wait_ge(sems["q_normed"], at("q_normed") + which[0])
                            sources = [qn[:, h, :] for h in range(G)]
                        elif what == "k":
                            if which[0] == 0:
                                pe.wait_ge(sems["k_normed"], start("k_normed") + 1)
                            sources = [k_norm[:, t, :] for t in range(4 * which[0], 4 * which[0] + 4)]
                        elif what == "wkv":
                            if which[0] == 0:
                                pe.wait_ge(wkv_loaded, 32 * ready)
                            sources = [wkv_raw[:, m, c * P:(c + 1) * P]
                                       for c in (2 * which[0], 2 * which[0] + 1) for m in range(2)]
                        elif what == "wq":
                            if which[0] == 0:
                                pe.wait_ge(wq_loaded, 16 * ready)
                            sources = [wq_raw[:, h, which[0] * P:(which[0] + 1) * P] for h in range(G)]
                        elif what == "wo":
                            if which[0] == 0:
                                pe.wait_ge(wo_loaded, 16 * (ready if plan is LAST_GROUP else ready - 1))
                            sources = [wo_raw[:, c, which[0] * P:(which[0] + 1) * P] for c in range(C)]
                        turn(base, unit, sources)

                    def q_part(s, c):
                        if c == 0:
                            if plan is PREPARE and s == NT:
                                pe.wait_ge(sems["lo_done"], base + unit_of["wq", C - 1] + 1)
                            elif plan is GROUP and s == NT:
                                pe.wait_ge(sems["lo_done"], base + unit_of["wq", C - 1] + 1)
                            if not (plan is PREPARE and s == NT):
                                pe.wait_ge(sems["q_normed"], at("q_normed") + s - 1)
                        tok = slice(s % NT * P, (s % NT + 1) * P)
                        last = split_product(q_ps[:], [((xnT_hi[:, c, tok], xnT_lo[:, c, tok]), (wqT_hi[:, c, :], wqT_lo[:, c, :]))],
                                             start=c == 0, stop=c == C - 1)
                        if c == C - 1:
                            last.then_inc(sems["q_full"], 1)

                    def scores(s, h):
                        L = (s + 1) * P
                        n = s * G + h
                        if h == 0 and s == 0:
                            pe.wait_ge(sems["lo_done"], base)
                        elif h == 0:
                            pe.wait_ge(sems["lo_done"], base + unit_of["q", s] + 1)
                        if L > 512:
                            pe.wait_ge(sems["s_max"], at("s_max") + n)
                        elif n >= 2:
                            pe.wait_ge(sems["s_max"], at("s_max") + n - 1)
                        for c in range(0, L, 512):
                            w = min(512, L - c)
                            at_col = 512 * (h % 2) if L <= 512 else c
                            last = split_product(s_ps[:, at_col:at_col + w],
                                                 [((qT_hi[:, s % 2, h, :], qT_lo[:, s % 2, h, :]),
                                                   (kT_hi[:, c:c + w], kT_lo[:, c:c + w]))])
                        last.then_inc(sems["s_full"], 1)

                    def kv(i):
                        if i == 0 and plan is PREPARE:
                            pe.wait_ge(sems["lo_done"], base + unit_of["wkv", C // 2 - 1] + 1)
                        elif i == 0:
                            pe.wait_ge(sems["s_max"], at("s_max") + NT * G)
                        if i >= 2:
                            pe.wait_ge(sems["kv_copied"], start("kv_copied") + i - 1)
                        for t in range(2):
                            tok = slice((2 * i + t) * P, (2 * i + t + 1) * P)
                            col = 512 * (i % 2) + t * 2 * HD
                            last = split_product(s_ps[:, col:col + 2 * HD],
                                                 [((xnT_hi[:, c, tok], xnT_lo[:, c, tok]), (wkvT_hi[:, c, :], wkvT_lo[:, c, :]))
                                                  for c in range(C)])
                        last.then_inc(sems["kv_full"], 1)

                    def values(s, j):
                        if s == 0:
                            pe.wait_ge(sems["v_lo_done"], at("v_lo_done"))
                        r = piece(s, j) % RING
                        pe.wait_ge(sems["lo_done"], base + unit_of["p", s, j] + 1)
                        last = split_product(o_ps[:], [((v_hi[:, j, :], v_lo[:, j, :]), (pT_hi[:, r, :], pT_lo[:, r, :]))],
                                             start=j == 0, stop=j == s)
                        if j == s:
                            last.then_inc(sems["o_full"], 1)

                    def y_product(s):
                        pe.wait_ge(sems["o_lo"], at("o_lo") + s + 1)
                        if s == 0:
                            pe.wait_ge(sems["lo_done"], base + unit_of["wo", G - 1] + 1)
                        else:
                            pe.wait_ge(sems["y_added"], at("y_added") + s)
                        split_product(y_ps[:], [((oT_hi[:, h, :], oT_lo[:, h, :]), (woT_hi[:, h, :], woT_lo[:, h, :]))
                                                for h in range(G)]).then_inc(sems["y_full"], 1)

                    follow({"turn": turn_what, "q_part": q_part, "scores": scores, "kv": kv, "values": values,
                            "y": y_product}, plan)

                run_plans(pe, run, b, True)

                def fat(name):
                    return ffn_at(name, b)

                for i in range(NT + 4):
                    if i < NT:
                        pe.wait_ge(sems["xn_ready"], fat("xn_ready") + i + 1)
                        turn(fat("lo_done"), UNIT_X[i], [x_normed[:, i, c * P:(c + 1) * P] for c in range(C)])
                    if 0 <= i - 1 < NT:
                        t = i - 1
                        pe.wait_ge(sems["lo_done"], fat("lo_done") + UNIT_X[t] + 1)
                        if t >= 2:
                            pe.wait_ge(sems["f_low"], fat("f_low") + t - 1)
                        for c in range(C):
                            last = nc.tensor.matmul((q_ps, o_ps)[t % 2][:, 0:P + NE], x_turned[:, t, c * P:(c + 1) * P],
                                                    arT[:, c, :], start=c == 0, stop=c == C - 1)
                        last.then_inc(sems["f_full"], 1)
                    if 0 <= i - 3 < NT:
                        t = i - 3
                        pe.wait_ge(sems["f_low"], fat("f_low") + t + 1)
                        turn(fat("lo_done"), UNIT_LOW[t], [low_gated[:, t, :]])
                    if 0 <= i - 4 < NT:
                        t = i - 4
                        pe.wait_ge(sems["lo_done"], fat("lo_done") + UNIT_LOW[t] + 1)
                        if t:
                            pe.wait_ge(sems["f_added"], fat("f_added") + t)
                        nc.tensor.matmul(y_ps[:], low_turned[:, t, :], bT[:], start=True, stop=True).then_inc(sems["f_out"], 1)


_INS = ["L0_attn_x", "L0_attn_Wq", "L0_attn_Wk", "L0_attn_Wv", "L0_attn_Wo", "L0_attn_q_norm_w", "L0_attn_k_norm_w",
        "L0_ffn_A", "L0_ffn_B", "L0_ffn_Wr", "L0_ffn_br"]


def kernel(**inputs):
    import concourse.bacc as bacc
    from concourse.bass_utils import run_bass_kernel_spmd

    nc = bacc.Bacc("TRN2", target_bir_lowering=False, num_devices=1)
    arrays, args = {}, []
    for name in _INS:
        a = np.ascontiguousarray(inputs[name])
        arrays[f"in_{name}"] = a
        args.append(nc.dram_tensor(f"in_{name}", a.shape, mybir.dt.from_np(a.dtype), kind="ExternalInput").ap())
    shape = inputs["L0_attn_x"].shape
    args.append(nc.dram_tensor("out_0", shape, F32, kind="ExternalOutput").ap())
    attention_lora_block(nc, *args)
    return run_bass_kernel_spmd(nc, [arrays], core_ids=[0]).results[0]["out_0"]
```

```python
import itertools
import math
from contextlib import ExitStack

import numpy as np

import concourse.bass as bass
from concourse import mybir

ALU = mybir.AluOpType
ACT = mybir.ActivationFunctionType
F32 = mybir.dt.float32
F32R = mybir.dt.float32r

P = 128
LN_EPS = 1e-5
RMS_EPS = 1e-6
NEG_INF = -1e30
LORA_SCALING = 32 / 16
BIG = 3e38

PREPARE_PLAN = (
    "turn.wkv.0 high.wkv.0 low.wkv.0 turn.wkv.1 high.wkv.1 turn.wq.0 low.wkv.1 turn.wq.1 turn.wq.2 high.wq.0 "
    "high.wq.1 kv.0 low.wq.0 table.0 low.wq.1 table.1 kv.1 high.wq.2 low.wq.2 turn.wq.3 high.wq.3 kv.2 low.wq.3 "
    "kv.3 q_part.8.0 inv_k q_part.8.1 norm_k q_part.8.2 split_v q_part.8.3 square_q.8 turn.k.0 inv_q.8 norm_q.8 "
    "turn.k.1 turn.q.8 q_part.9.0 q_part.9.1 high.k.0 table.2 q_part.9.2 q_part.9.3 table.3 low.k.0 high.k.1 "
    "high.q.8 low.k.1 square_q.9 low.q.8 inv_q.9 "
)
GROUP_PLAN = (
    "norm_q.1 turn.wo.0 high.wo.0 low.wo.0 scores.0.0 max.0.0 turn.wo.1 high.wo.1 scores.0.1 turn.wo.2 max.0.1 "
    "q_part.2.0 exp.0.0 scores.0.2 turn.q.1 low.wo.1 high.wo.2 scores.0.3 max.0.2 low.wo.2 high.q.1 exp.0.1 "
    "turn.wo.3 low.q.1 q_part.2.1 invert.0.0 normalise.0.0 high.wo.3 q_part.2.2 q_part.2.3 normalise.0.1 max.0.3 "
    "exp.0.2 invert.0.1 normalise.0.2 normalise.0.3 "
    "scores.1.0 exp.0.3 scores.1.1 low.wo.3 turn.p.0.0 max.1.0 square_q.2 scores.1.2 inv_q.2 high.p.0.0 exp.1.0 "
    "normalise.1.0 max.1.1 low.p.0.0 normalise.1.1 exp.1.1 normalise.1.2 norm_q.2 scores.1.3 max.1.2 values.0.0 "
    "exp.1.2 invert.1.0 max.1.3 turn.q.2 q_part.3.0 high.q.2 exp.1.3 low.q.2 invert.1.1 q_part.3.1 split_o.0 "
    "q_part.3.2 q_part.3.3 "
    "scores.2.0 turn.p.1.0 square_q.3 normalise.1.3 high.p.1.0 y.0 max.2.0 low.p.1.0 add_y.0 turn.p.1.1 "
    "scores.2.1 high.p.1.1 max.2.1 inv_q.3 low.p.1.1 scores.2.2 norm_q.3 values.1.0 scores.2.3 exp.2.0 "
    "normalise.2.0 max.2.2 normalise.2.1 max.2.3 normalise.2.2 exp.2.1 values.1.1 exp.2.2 turn.q.3 high.q.3 "
    "invert.2.0 q_part.4.0 q_part.4.1 q_part.4.2 low.q.3 split_o.1 invert.2.1 exp.2.3 normalise.2.3 q_part.4.3 "
    "scores.3.0 max.3.0 square_q.4 add_y.1 y.1 turn.p.2.0 inv_q.4 norm_q.4 turn.p.2.1 high.p.2.0 low.p.2.0 "
    "high.p.2.1 low.p.2.1 scores.3.1 max.3.1 turn.p.2.2 scores.3.2 turn.q.4 normalise.3.0 max.3.2 values.2.0 "
    "exp.3.0 high.p.2.2 exp.3.1 scores.3.3 normalise.3.1 low.p.2.2 max.3.3 values.2.1 high.q.4 q_part.5.0 "
    "values.2.2 normalise.3.2 invert.3.0 q_part.5.1 q_part.5.2 low.q.4 exp.3.2 "
    "scores.4.0 split_o.2 exp.3.3 q_part.5.3 invert.3.1 max.4.0 y.2 add_y.2 turn.p.3.0 exp.4.0 scores.4.1 "
    "normalise.3.3 high.p.3.0 low.p.3.0 square_q.5 turn.wkv.0 high.wkv.0 turn.p.3.1 values.3.0 high.p.3.1 inv_q.5 "
    "max.4.1 low.wkv.0 low.p.3.1 scores.4.2 turn.p.3.2 max.4.2 high.p.3.2 norm_q.5 exp.4.1 turn.p.3.3 "
    "normalise.4.0 low.p.3.2 invert.4.0 values.3.1 normalise.4.1 scores.4.3 normalise.4.2 max.4.3 high.p.3.3 "
    "turn.q.5 values.3.2 low.p.3.3 q_part.6.0 values.3.3 invert.4.1 q_part.6.1 exp.4.2 exp.4.3 q_part.6.2 "
    "high.q.5 low.q.5 "
    "scores.5.0 split_o.3 q_part.6.3 turn.p.4.0 max.5.0 square_q.6 high.p.4.0 y.3 scores.5.1 low.p.4.0 add_y.3 "
    "turn.p.4.1 max.5.1 normalise.4.3 high.p.4.1 norm_q.6 low.p.4.1 turn.p.4.2 high.p.4.2 values.4.0 inv_q.6 "
    "exp.5.0 turn.wkv.1 q_part.7.0 scores.5.2 exp.5.1 low.p.4.2 values.4.1 max.5.2 high.wkv.1 turn.p.4.3 "
    "values.4.2 normalise.5.0 turn.p.4.4 invert.5.0 high.p.4.3 scores.5.3 high.p.4.4 low.wkv.1 low.p.4.3 turn.q.6 "
    "low.p.4.4 high.q.6 normalise.5.1 max.5.3 values.4.3 values.4.4 exp.5.2 q_part.7.1 low.q.6 "
    "scores.6.0 invert.5.1 q_part.7.2 split_o.4 q_part.7.3 y.4 max.6.0 exp.5.3 normalise.5.2 turn.p.5.0 "
    "high.p.5.0 turn.p.5.1 add_y.4 normalise.5.3 high.p.5.1 inv_q.7 low.p.5.0 exp.6.0 scores.6.1 turn.wq.0 "
    "high.wq.0 low.p.5.1 turn.wq.1 turn.p.5.2 max.6.1 values.5.0 high.wq.1 high.p.5.2 low.wq.0 low.wq.1 "
    "square_q.7 exp.6.1 scores.6.2 turn.p.5.3 normalise.6.0 low.p.5.2 turn.wq.2 values.5.1 high.p.5.3 max.6.2 "
    "high.wq.2 low.p.5.3 norm_q.7 turn.p.5.4 values.5.2 low.wq.2 high.p.5.4 invert.6.0 low.p.5.4 turn.wq.3 "
    "high.wq.3 low.wq.3 normalise.6.1 scores.6.3 turn.p.5.5 max.6.3 turn.q.7 normalise.6.2 values.5.3 exp.6.2 "
    "high.p.5.5 high.q.7 low.p.5.5 low.q.7 q_part.8.0 values.5.4 values.5.5 split_o.5 invert.6.1 q_part.8.1 "
    "scores.7.0 q_part.8.2 exp.6.3 y.5 max.7.0 normalise.6.3 turn.p.6.0 turn.p.6.1 turn.p.6.2 high.p.6.0 "
    "scores.7.1 low.p.6.0 high.p.6.1 low.p.6.1 exp.7.0 max.7.1 q_part.8.3 values.6.0 values.6.1 scores.7.2 "
    "high.p.6.2 turn.p.6.3 add_y.5 invert.7.0 square_q.8 exp.7.1 turn.p.6.4 high.p.6.3 high.p.6.4 normalise.7.0 "
    "values.6.2 low.p.6.2 inv_q.8 turn.p.6.5 max.7.2 high.p.6.5 low.p.6.3 scores.7.3 low.p.6.4 exp.7.2 values.6.3 "
    "low.p.6.5 norm_q.8 turn.p.6.6 high.p.6.6 turn.q.8 max.7.3 values.6.4 normalise.7.1 exp.7.3 low.p.6.6 "
    "values.6.5 invert.7.1 high.q.8 values.6.6 low.q.8 split_o.6 kv.0 add_y.6 y.6 "
    "turn.p.7.0 high.p.7.0 table.0 low.p.7.0 turn.p.7.1 normalise.7.2 high.p.7.1 turn.p.7.2 high.p.7.2 low.p.7.1 "
    "kv.1 values.7.0 values.7.1 turn.p.7.3 normalise.7.3 high.p.7.3 turn.p.7.4 low.p.7.2 values.7.2 turn.p.7.5 "
    "high.p.7.4 kv.2 low.p.7.3 low.p.7.4 high.p.7.5 kv.3 values.7.3 low.p.7.5 turn.p.7.6 high.p.7.6 values.7.4 "
    "inv_k turn.p.7.7 q_part.9.0 high.p.7.7 table.1 low.p.7.6 values.7.5 low.p.7.7 norm_k q_part.9.1 values.7.6 "
    "values.7.7 split_o.7 q_part.9.2 turn.k.0 turn.k.1 split_v q_part.9.3 high.k.0 low.k.0 table.2 high.k.1 "
    "low.k.1 y.7 square_q.9 inv_q.9 table.3 add_y.7 "
)
LAST_GROUP_PLAN = (
    "turn.wo.0 high.wo.0 norm_q.1 scores.0.0 turn.wo.1 scores.0.1 max.0.0 max.0.1 high.wo.1 turn.wo.2 low.wo.0 "
    "scores.0.2 low.wo.1 q_part.2.0 turn.q.1 high.wo.2 scores.0.3 exp.0.0 max.0.2 high.q.1 turn.wo.3 low.wo.2 "
    "q_part.2.1 q_part.2.2 invert.0.0 low.q.1 normalise.0.0 normalise.0.1 max.0.3 exp.0.1 invert.0.1 q_part.2.3 "
    "high.wo.3 exp.0.2 exp.0.3 "
    "scores.1.0 low.wo.3 square_q.2 scores.1.1 max.1.0 normalise.0.2 turn.p.0.0 normalise.0.3 exp.1.0 inv_q.2 "
    "high.p.0.0 max.1.1 low.p.0.0 scores.1.2 scores.1.3 norm_q.2 exp.1.1 invert.1.0 max.1.2 exp.1.2 values.0.0 "
    "normalise.1.0 turn.q.2 q_part.3.0 normalise.1.1 max.1.3 q_part.3.1 high.q.2 exp.1.3 q_part.3.2 low.q.2 "
    "split_o.0 "
    "scores.2.0 y.0 invert.1.1 turn.p.1.0 q_part.3.3 max.2.0 scores.2.1 normalise.1.2 high.p.1.0 add_y.0 "
    "x_stats.0 scores.2.2 square_q.3 turn.p.1.1 normalise.1.3 max.2.1 low.p.1.0 max.2.2 exp.2.0 scores.2.3 "
    "x_moments.0 high.p.1.1 low.p.1.1 values.1.0 inv_q.3 norm_q.3 exp.2.1 invert.2.0 x_rstd.0 values.1.1 max.2.3 "
    "normalise.2.0 turn.q.3 split_o.1 high.q.3 normalise.2.1 q_part.4.0 low.q.3 q_part.4.1 q_part.4.2 invert.2.1 "
    "exp.2.2 q_part.4.3 normalise.2.2 "
    "scores.3.0 y.1 turn.p.2.0 max.3.0 normalise.2.3 exp.2.3 square_q.4 high.p.2.0 inv_q.4 add_y.1 norm_q.4 "
    "turn.p.2.1 x_stats.1 low.p.2.0 turn.p.2.2 scores.3.1 high.p.2.1 scores.3.2 low.p.2.1 q_part.5.0 max.3.1 "
    "max.3.2 high.p.2.2 x_moments.1 values.2.0 x_rstd.1 turn.q.4 values.2.1 scores.3.3 exp.3.0 exp.3.1 low.p.2.2 "
    "invert.3.0 normalise.3.0 high.q.4 q_part.5.1 low.q.4 exp.3.2 values.2.2 max.3.3 "
    "scores.4.0 q_part.5.2 invert.3.1 normalise.3.1 split_o.2 q_part.5.3 exp.3.3 max.4.0 y.2 normalise.3.2 "
    "turn.p.3.0 normalise.3.3 square_q.5 scores.4.1 add_y.2 x_stats.2 x_moments.2 high.p.3.0 turn.p.3.1 exp.4.0 "
    "high.p.3.1 low.p.3.0 turn.p.3.2 values.3.0 x_rstd.2 max.4.1 scores.4.2 exp.4.1 high.p.3.2 low.p.3.1 "
    "values.3.1 inv_q.5 turn.p.3.3 max.4.2 invert.4.0 norm_q.5 high.p.3.3 low.p.3.2 scores.4.3 exp.4.2 max.4.3 "
    "invert.4.1 turn.q.5 normalise.4.0 exp.4.3 q_part.6.0 values.3.2 q_part.6.1 q_part.6.2 normalise.4.1 "
    "normalise.4.2 low.p.3.3 values.3.3 q_part.6.3 high.q.5 low.q.5 "
    "scores.5.0 split_o.3 square_q.6 normalise.4.3 turn.p.4.0 y.3 high.p.4.0 max.5.0 turn.p.4.1 high.p.4.1 "
    "low.p.4.0 scores.5.1 add_y.3 x_stats.3 x_moments.3 turn.p.4.2 max.5.1 low.p.4.1 values.4.0 x_rstd.3 "
    "turn.p.4.3 high.p.4.2 scores.5.2 inv_q.6 low.p.4.2 values.4.1 values.4.2 max.5.2 exp.5.0 high.p.4.3 exp.5.1 "
    "turn.p.4.4 invert.5.0 scores.5.3 low.p.4.3 norm_q.6 turn.q.6 high.p.4.4 normalise.5.0 high.q.6 low.p.4.4 "
    "normalise.5.1 exp.5.2 values.4.3 values.4.4 max.5.3 low.q.6 q_part.7.0 split_o.4 q_part.7.1 q_part.7.2 "
    "invert.5.1 normalise.5.2 "
    "scores.6.0 max.6.0 exp.5.3 y.4 q_part.7.3 add_y.4 turn.p.5.0 x_stats.4 exp.6.0 high.p.5.0 normalise.5.3 "
    "low.p.5.0 turn.p.5.1 x_moments.4 x_rstd.4 scores.6.1 max.6.1 turn.p.5.2 high.p.5.1 square_q.7 low.p.5.1 "
    "values.5.0 inv_q.7 turn.p.5.3 scores.6.2 high.p.5.2 low.p.5.2 exp.6.1 values.5.1 high.p.5.3 max.6.2 "
    "invert.6.0 norm_q.7 normalise.6.0 turn.p.5.4 high.p.5.4 values.5.2 normalise.6.1 low.p.5.3 low.p.5.4 "
    "turn.p.5.5 high.p.5.5 scores.6.3 values.5.3 turn.q.7 exp.6.2 low.p.5.5 values.5.4 max.6.3 high.q.7 low.q.7 "
    "values.5.5 invert.6.1 "
    "scores.7.0 exp.6.3 split_o.5 max.7.0 normalise.6.2 y.5 turn.p.6.0 exp.7.0 high.p.6.0 turn.p.6.1 scores.7.1 "
    "low.p.6.0 turn.p.6.2 high.p.6.1 high.p.6.2 normalise.6.3 low.p.6.1 max.7.1 low.p.6.2 values.6.0 values.6.1 "
    "exp.7.1 scores.7.2 turn.p.6.3 add_y.5 turn.p.6.4 high.p.6.3 high.p.6.4 x_stats.5 values.6.2 max.7.2 "
    "x_moments.5 invert.7.0 low.p.6.3 turn.p.6.5 scores.7.3 values.6.3 exp.7.2 x_rstd.5 normalise.7.0 turn.p.6.6 "
    "high.p.6.5 low.p.6.4 values.6.4 max.7.3 low.p.6.5 high.p.6.6 low.p.6.6 values.6.5 values.6.6 split_o.6 "
    "normalise.7.1 y.6 invert.7.1 exp.7.3 "
    "turn.p.7.0 add_y.6 x_stats.6 turn.p.7.1 normalise.7.2 turn.p.7.2 x_moments.6 high.p.7.0 x_rstd.6 high.p.7.1 "
    "low.p.7.0 values.7.0 turn.p.7.3 low.p.7.1 high.p.7.2 low.p.7.2 values.7.1 turn.p.7.4 high.p.7.3 values.7.2 "
    "turn.p.7.5 low.p.7.3 values.7.3 high.p.7.4 low.p.7.4 turn.p.7.6 x_norm.0 values.7.4 high.p.7.5 high.p.7.6 "
    "low.p.7.5 turn.p.7.7 low.p.7.6 normalise.7.3 turn.x.0 high.p.7.7 values.7.5 low.p.7.7 values.7.6 low.x.0 "
    "x_norm.1 values.7.7 logits.0 split_o.7 f_max.0 f_exp.0 turn.x.1 x_norm.2 y.7 turn.x.2 f_inv.0 low.x.1 "
    "add_y.7 logits.1 x_stats.7 low.x.2 x_moments.7 x_rstd.7 f_gate.0 f_max.1 f_exp.1 f_low.0 f_inv.1 turn.lora.0 "
    "f_gate.1 x_norm.3 f_low.1 low.lora.0 logits.2 turn.x.3 f_out.0 low.x.3 f_max.2 turn.lora.1 add_f.0 f_exp.2 "
    "logits.3 f_inv.2 x_norm.4 f_gate.2 turn.x.4 low.lora.1 f_low.2 turn.lora.2 f_max.3 f_exp.3 low.x.4 f_out.1 "
    "logits.4 x_norm.5 turn.x.5 f_inv.3 low.lora.2 f_gate.3 x_norm.6 f_max.4 add_f.1 low.x.5 f_exp.4 f_out.2 "
    "f_inv.4 f_low.3 turn.lora.3 logits.5 f_gate.4 f_low.4 add_f.2 low.lora.3 f_max.5 f_exp.5 turn.x.6 x_norm.7 "
    "f_inv.5 turn.lora.4 f_out.3 turn.x.7 low.x.6 logits.6 low.lora.4 add_f.3 low.x.7 f_gate.5 f_max.6 f_low.5 "
    "f_out.4 f_exp.6 turn.lora.5 logits.7 f_inv.6 f_gate.6 add_f.4 low.lora.5 f_low.6 f_max.7 f_exp.7 f_inv.7 "
    "f_out.5 turn.lora.6 add_f.5 low.lora.6 f_gate.7 f_low.7 f_out.6 turn.lora.7 add_f.6 low.lora.7 f_out.7 "
    "add_f.7 "
)


def alibi_slopes(n_heads):
    start = 2 ** (-2 ** (-(math.log2(n_heads) - 3)))
    return np.array([start * start ** i for i in range(n_heads)], dtype=np.float32)


def attention_lora_block(nc, x, Wq, Wk, Wv, Wo, q_norm_w, k_norm_w, A, B, Wr, br, out):
    NB, S, DM = x.shape
    HD = q_norm_w.shape[0]
    H = Wq.shape[0] // HD
    NG = Wk.shape[0] // HD
    G = H // NG
    NE, RK, _ = A.shape
    NT = S // P
    C = DM // P
    W512 = G * HD
    assert HD == P and W512 == 512 and DM == 512 and NE * RK == P and S == 1024
    slopes = alibi_slopes(H)
    CARRIERS = 16
    RING = 3

    def read(text):
        return [tuple(int(w) if w.isdigit() else w for w in item.split(".")) for item in text.split()]

    PREPARE, GROUP, LAST_GROUP = read(PREPARE_PLAN), read(GROUP_PLAN), read(LAST_GROUP_PLAN)

    def signals(kind):
        return tuple(sum(x[0] == kind for x in plan) for plan in (PREPARE, GROUP, LAST_GROUP))

    q_counts = tuple(sum(x[0] == "q_part" and x[2] == C - 1 for x in plan) for plan in (PREPARE, GROUP, LAST_GROUP))
    COUNTS = {
        "turned": (3, NT, *signals("turn")),
        "hi_done": (0, NT, *signals("high")),
        "lo_done": (3, NT, *signals("low")),
        "ln_stats": (0, NT, *signals("x_stats")), "ln_moments": (0, NT, *signals("x_moments")),
        "ln_var_eps": (0, 2, *signals("x_rstd")), "ln_rstd": (0, 2, *signals("x_rstd")),
        "xn_ready": (0, NT, *signals("x_norm")),
        "bias_ready": (0, 0, *signals("table")),
        "kv_full": (0, 0, *signals("kv")), "kv_squares": (0, 0, *signals("kv")),
        "kv_copied": (0, 0, *signals("kv")),
        "k_sum_eps": (0, 0, *signals("inv_k")), "k_inv": (0, 0, *signals("inv_k")),
        "k_normed": (0, 0, *signals("norm_k")),
        "v_hi_done": (0, 0, *signals("split_v")), "v_lo_done": (0, 0, *signals("split_v")),
        "q_full": (0, 0, *q_counts), "q_squares": (0, 0, *q_counts), "q_sum_eps": (0, 0, *q_counts),
        "q_inv": (0, 0, *q_counts), "q_normed": (0, 0, *signals("norm_q")),
        "s_full": (0, 0, *signals("scores")), "s_max": (0, 0, *signals("scores")),
        "p_exp": (0, 0, *signals("exp")), "p_inv": (0, 0, *signals("invert")),
        "p_ready": (0, 0, *signals("normalise")),
        "o_full": (0, 0, *signals("y")), "o_hi": (0, 0, *signals("y")), "o_lo": (0, 0, *signals("y")),
        "y_full": (0, 0, *signals("y")), "y_added": (0, 0, *signals("y")),
        "f_full": (0, 0, *signals("logits")), "f_max": (0, 0, *signals("f_max")), "f_exp": (0, 0, *signals("f_exp")),
        "f_inv": (0, 0, *signals("f_inv")), "f_gate": (0, 0, *signals("f_gate")), "f_low": (0, 0, *signals("f_low")),
        "f_out": (0, 0, *signals("f_out")), "f_added": (0, 0, *signals("add_f")),
    }

    def batch_at(name, b):
        pro, ln, prep, grp, last = COUNTS[name]
        return b * (ln + prep + (NG - 1) * grp + last) + pro

    def ln_at(name, b):
        return batch_at(name, b)

    def prepare_at(name, b):
        return batch_at(name, b) + COUNTS[name][1]

    def group_at(name, b, g):
        pro, ln, prep, grp, last = COUNTS[name]
        return batch_at(name, b) + g * grp + (ln + prep)

    def units(plan):
        return {x[1:]: n for n, x in enumerate(x for x in plan if x[0] == "turn")}

    def high_units(plan):
        return {x[1:]: n for n, x in enumerate(x for x in plan if x[0] == "high")}

    def piece(s, j):
        return s * (s + 1) // 2 + j

    def scores_col(s, h):
        L = (s + 1) * P
        return 512 * (h % 2) if L <= 512 else 512 - min(512, L - 256)

    def follow(work, plan):
        for kind, *what in plan:
            if kind in work:
                work[kind](*what)

    with ExitStack() as ctx:
        def sb(name, shape, dt=F32):
            return ctx.enter_context(nc.sbuf_tensor(name, shape, dt))

        def psum(name, shape):
            return ctx.enter_context(nc.psum_tensor(name, shape, F32))

        def sem(name):
            return ctx.enter_context(nc.semaphore(name))

        xnT_hi = sb("xnT_hi", [P, C, S], F32R)
        xnT_lo = sb("xnT_lo", [P, C, S], F32R)
        y = sb("y", [P, NT, DM])
        wqT_hi = sb("wqT_hi", [P, C, W512], F32R)
        wqT_lo = sb("wqT_lo", [P, C, W512], F32R)
        wkvT_hi = sb("wkvT_hi", [P, C, 2 * HD], F32R)
        wkvT_lo = sb("wkvT_lo", [P, C, 2 * HD], F32R)
        woT_hi = sb("woT_hi", [P, G, DM], F32R)
        woT_lo = sb("woT_lo", [P, G, DM], F32R)
        wq_raw = sb("wq_raw", [P, G, DM])
        wkv_raw = sb("wkv_raw", [P, 2, DM])
        wo_raw = sb("wo_raw", [P, C, W512])
        kT_hi = sb("kT_hi", [P, S], F32R)
        kT_lo = sb("kT_lo", [P, S], F32R)
        v_hi = sb("v_hi", [P, NT, HD], F32R)
        v_lo = sb("v_lo", [P, NT, HD], F32R)
        rel = sb("rel", [P, S])
        bias = sb("bias", [P, G, S])
        probs = sb("probs", [P, 2, G, S])
        qn = sb("qn", [P, G, HD])
        qT_hi = sb("qT_hi", [P, 2, G, P], F32R)
        qT_lo = sb("qT_lo", [P, 2, G, P], F32R)
        pT_hi = sb("pT_hi", [P, RING, G * P], F32R)
        pT_lo = sb("pT_lo", [P, RING, G * P], F32R)
        oT_hi = sb("oT_hi", [P, G, P], F32R)
        oT_lo = sb("oT_lo", [P, G, P], F32R)
        arT = sb("arT", [P, C, P + NE])
        bT = sb("bT", [P, DM])
        ident = sb("ident", [P, P])
        slope_row = sb("slope_row", [P, H])
        minus_half = sb("minus_half", [P, NT])
        ln_eps = sb("ln_eps", [P, NT // 2])
        rms_eps = sb("rms_eps", [P, NT])
        scratch = sb("scratch", [P, CARRIERS, 1])
        wq_norm = sb("wq_norm", [P, 1])
        wk_norm = sb("wk_norm", [P, 1])
        wk_scaled = sb("wk_scaled", [P, 1])
        br_row = sb("br_row", [P, NE])
        stats = sb("stats", [P, NT, 6])
        moments = sb("moments", [P, NT, 2])
        var_eps = sb("var_eps", [P, NT])
        rstd = sb("rstd", [P, NT])
        k_sum = sb("k_sum", [P, NT])
        k_sum_eps_t = sb("k_sum_eps_t", [P, NT])
        k_inv_t = sb("k_inv_t", [P, NT])
        q_sum = sb("q_sum", [P, G])
        q_sum_eps_t = sb("q_sum_eps_t", [P, G])
        q_inv_t = sb("q_inv_t", [P, G])
        neg_max = sb("neg_max", [P, 2, G])
        p_sum = sb("p_sum", [P, 2, G])
        p_inv_t = sb("p_inv_t", [P, 2, G])
        f_neg_max = sb("f_neg_max", [P, NT])
        f_sum = sb("f_sum", [P, NT])
        f_inv_t = sb("f_inv_t", [P, NT])

        slots = probs[:].rearrange("p a h s -> p (a h) s")
        kv_raw = probs[:, 0, 0:2, :].rearrange("p a (t d) -> p (a t) d", d=2 * HD)
        k_norm = probs[:, 0, 2, :].rearrange("p (t d) -> p t d", d=HD)
        x_normed = slots[:, :, 0:DM]
        x_turned = slots[:, :, DM:2 * DM]
        low_gated = bias[:, 0, :].rearrange("p (t n) -> p t n", n=P)
        low_turned = bias[:, 1, :].rearrange("p (t n) -> p t n", n=P)
        a_raw = bias[:, 0, 0:DM]
        wr_raw = bias[0:NE, 1, 0:DM]
        b_raw = bias[:, 2, 0:DM].rearrange("p (h o r) -> p h o r", o=C, r=RK)
        b_sorted = bias[:, 3, 0:DM].rearrange("p (o h r) -> p o h r", o=C, r=RK)
        f_logits, f_weights, f_gates = (
            bias[:, 2, i * NT * NE:(i + 1) * NT * NE].rearrange("p (t n) -> p t n", n=NE) for i in range(3))

        s_ps = psum("s_ps", [P, 1024])
        turn_ps = [psum(f"turn_ps{i}", [P, 512]) for i in range(RING)]
        q_ps = psum("q_ps", [P, 512])
        o_ps = psum("o_ps", [P, 512])
        y_ps = psum("y_ps", [P, 512])

        sems = {name: sem(name) for name in COUNTS}
        ident_ready = sem("ident_ready")
        rel_ready = sem("rel_ready")
        tables_ready = sem("tables_ready")
        wk_scaled_ready = sem("wk_scaled_ready")
        pool_step = sem("pool_step")
        small_loaded = sem("small_loaded")
        ffn_loaded = sem("ffn_loaded")
        b_sorted_ready = sem("b_sorted_ready")
        x_loaded = [sem(f"x_loaded{i}") for i in range(NT)]
        wkv_loaded = sem("wkv_loaded")
        wq_loaded = sem("wq_loaded")
        wo_loaded = sem("wo_loaded")
        stored = [sem("stored_even"), sem("stored_odd")]

        block = ctx.enter_context(nc.Block())

        def run_plans(engine, run, b, with_group=False):
            def prepared(name):
                return prepare_at(name, b) + (COUNTS[name][2] - COUNTS[name][3])

            run(PREPARE, prepared, lambda name: prepare_at(name, b), *([0] if with_group else []))
            with engine.Fori(0, NG - 1) as g:
                run(GROUP, lambda name: group_at(name, b, g), lambda name: group_at(name, b, g),
                    *([g + 1] if with_group else []))
            run(LAST_GROUP, lambda name: group_at(name, b, NG - 1), lambda name: group_at(name, b, NG - 1),
                *([NG - 1] if with_group else []))

        @block.sync
        def _(sp):
            x_v = x.rearrange("b (t p) d -> b p t d", p=P)
            out_v = out.rearrange("b (t p) d -> b p t d", p=P)
            wq_v = Wq.rearrange("(g h p) d -> g p h d", h=G, p=P)
            wk_v = Wk.rearrange("(g p) d -> g p d", p=P)
            wv_v = Wv.rearrange("(g p) d -> g p d", p=P)
            wo_v = Wo.rearrange("(c p) (g n) -> g p c n", p=P, n=W512)

            def load_wqkv(g):
                sp.dma_start(wkv_raw[:, 0, :], wk_v[g]).then_inc(wkv_loaded, 16)
                sp.dma_start(wkv_raw[:, 1, :], wv_v[g]).then_inc(wkv_loaded, 16)
                sp.dma_start(wq_raw[:], wq_v[g]).then_inc(wq_loaded, 16)

            def load_wo(g):
                sp.dma_start(wo_raw[:], wo_v[g]).then_inc(wo_loaded, 16)

            wo_turned = units(GROUP)["wo", G - 1] + 1

            def load_next(b, g, following):
                sp.wait_ge(sems["turned"], group_at("turned", b, g))
                load_wqkv(following)
                sp.wait_ge(sems["turned"], group_at("turned", b, g) + wo_turned)
                load_wo(following)

            def load_x(b, t):
                sp.dma_start(y[:, t, :], x_v[b, :, t, :]).then_inc(x_loaded[t], 16)

            for t in range(NT):
                load_x(0, t)
            load_wqkv(0)
            load_wo(0)
            for b in range(NB):
                with sp.Fori(0, NG - 1) as g:
                    load_next(b, g, g + 1)
                if b < NB - 1:
                    load_next(b, NG - 1, 0)
                for t in range(NT + 1):
                    if t < NT:
                        sp.wait_ge(sems["f_added"], group_at("f_added", b, NG - 1) + t + 1)
                        sp.dma_start(out_v[b, :, t, :], y[:, t, :]).then_inc(stored[t % 2], 16)
                    if t:
                        sp.wait_ge(stored[(t - 1) % 2], 16 * (NT // 2 * b + (t - 1) // 2 + 1))
                        if b < NB - 1:
                            load_x(b + 1, t - 1)

        @block.scalar
        def _(act):
            act.dma_start(wk_norm[:], k_norm_w.rearrange("(p a) -> p a", a=1)).then_inc(small_loaded, 16)
            act.dma_start(wq_norm[:], q_norm_w.rearrange("(p a) -> p a", a=1)).then_inc(small_loaded, 16)
            act.dma_start(br_row[:], br.rearrange("(a n) -> a n", a=1).broadcast_to((P, NE))).then_inc(small_loaded, 16)
            act.dma_start(a_raw, A.rearrange("h r d -> (h r) d")).then_inc(ffn_loaded, 16)
            act.dma_start(wr_raw, Wr).then_inc(ffn_loaded, 16)
            act.dma_start(b_raw, B.rearrange("h (p o) r -> p h o r", o=C)).then_inc(ffn_loaded, 16)
            act.wait_ge(ffn_loaded, 48)
            nc.scalar.activation(b_sorted.rearrange("p o h r -> p h o r"), b_raw, ACT.Copy).then_inc(b_sorted_ready, 1)
            act.wait_ge(sems["turned"], 1)
            nc.scalar.activation(arT[:, :, 0:P], turn_ps[0][:].rearrange("p (c n) -> p c n", c=C),
                                 ACT.Copy).then_inc(sems["lo_done"], 1)
            act.wait_ge(sems["turned"], 2)
            nc.scalar.activation(arT[:, :, P:P + NE], turn_ps[1][:, 0:C * NE].rearrange("p (c n) -> p c n", c=C),
                                 ACT.Copy).then_inc(sems["lo_done"], 1)
            act.wait_ge(sems["turned"], 3)
            nc.scalar.activation(bT[:].rearrange("p (n o) -> p o n", o=C), turn_ps[2][:].rearrange("p (o n) -> p o n", o=C),
                                 ACT.Copy).then_inc(sems["lo_done"], 1)
            act.wait_ge(small_loaded, 48)
            act.wait_ge(wk_scaled_ready, 1)

            def high(base, unit, target, source, scale=None):
                act.wait_ge(sems["turned"], base + unit + 1)
                if scale is None:
                    nc.scalar.activation(target, source, ACT.Copy).then_inc(sems["hi_done"], 1)
                else:
                    nc.scalar.activation(target, source, ACT.Copy, scale=scale).then_inc(sems["hi_done"], 1)

            with act.Fori(0, NB) as b:
                base = ln_at("turned", b)
                for t in range(NT):
                    high(base, t, xnT_hi[:, :, t * P:(t + 1) * P],
                         turn_ps[t % RING][:].rearrange("p (c n) -> p c n", c=C))

                def run(plan, at, start):
                    unit_of = units(plan)
                    base = start("turned")

                    def turn(what, *which):
                        unit = unit_of[(what, *which)]
                        bank = turn_ps[unit % RING][:]
                        if what == "p":
                            high(base, unit, pT_hi[:, piece(*which) % RING, :], bank)
                        elif what == "q":
                            high(base, unit, qT_hi[:, which[0] % 2].rearrange("p h n -> p (h n)"), bank, wq_norm[:])
                        elif what == "k":
                            high(base, unit, kT_hi[:, which[0] * 512:(which[0] + 1) * 512], bank, wk_scaled[:])
                        elif what == "wkv":
                            i = which[0]
                            high(base, unit, wkvT_hi[:, 2 * i:2 * i + 2, :].rearrange("p c n -> p (c n)"), bank)
                        elif what == "wq":
                            high(base, unit, wqT_hi[:, which[0], :], bank)
                        elif what == "wo":
                            high(base, unit, woT_hi[:, which[0], :], bank)

                    def exp(s, h):
                        n = s * G + h
                        L = (s + 1) * P
                        act.wait_ge(sems["s_max"], at("s_max") + n + 1)
                        row = probs[:, s % 2, h, 0:L]
                        nc.scalar.activation(row, row, ACT.Exp, bias=neg_max[:, s % 2, h:h + 1], scale=-1.0,
                                             accum_out=p_sum[:, s % 2, h:h + 1]).then_inc(sems["p_exp"], 1)

                    def square_q(s):
                        act.wait_ge(sems["q_full"], at("q_full") + s - 1)
                        for h in range(G):
                            last = nc.scalar.activation(qn[:, h, :], q_ps[:, h * HD:(h + 1) * HD], ACT.Square,
                                                        accum_out=q_sum[:, h:h + 1])
                        last.then_inc(sems["q_squares"], 1)

                    def kv(i):
                        act.wait_ge(sems["kv_full"], start("kv_full") + i + 1)
                        for t in range(2):
                            last = nc.scalar.activation(k_norm[:, 2 * i + t, :], s_ps[:, 512 * (i % 2) + t * 2 * HD:][:, 0:HD],
                                                        ACT.Square, accum_out=k_sum[:, 2 * i + t:2 * i + t + 1])
                        last.then_inc(sems["kv_squares"], 1)

                    def split_v():
                        act.wait_ge(sems["kv_copied"], start("kv_copied") + NT // 2)
                        if plan is GROUP:
                            act.wait_ge(sems["o_full"], at("o_full") + NT)
                        nc.scalar.activation(v_hi[:], kv_raw[:, :, HD:2 * HD], ACT.Copy).then_inc(sems["v_hi_done"], 1)

                    def split_o(s):
                        act.wait_ge(sems["o_full"], at("o_full") + s + 1)
                        nc.scalar.activation(oT_hi[:].rearrange("p h n -> p (h n)"), o_ps[:],
                                             ACT.Copy).then_inc(sems["o_hi"], 1)

                    def f_exp(t):
                        act.wait_ge(sems["f_max"], at("f_max") + t + 1)
                        nc.scalar.activation(f_weights[:, t, :], f_logits[:, t, :], ACT.Exp, bias=f_neg_max[:, t:t + 1],
                                             scale=-1.0, accum_out=f_sum[:, t:t + 1]).then_inc(sems["f_exp"], 1)

                    follow({"high": turn, "exp": exp, "square_q": square_q, "kv": kv, "split_v": split_v,
                            "split_o": split_o, "f_exp": f_exp}, plan)

                run_plans(act, run, b)

        @block.gpsimd
        def _(pool):
            nc.gpsimd.memset(ident[:], 0.0).then_inc(pool_step, 1)
            nc.gpsimd.iota(rel[:], [[1, S]], base=-(S - P), channel_multiplier=-1,
                           allow_small_or_imprecise_dtypes=True).then_inc(pool_step, 1)
            pool.wait_ge(pool_step, 2)
            nc.gpsimd.affine_select(out=ident[:], in_=ident[:], compare_op=ALU.not_equal, fill=1.0, base=0,
                                    pattern=[[-1, P]], channel_multiplier=1).then_inc(ident_ready, 1)
            nc.gpsimd.affine_select(out=rel[:], in_=rel[:], compare_op=ALU.is_ge, fill=NEG_INF, base=S - P,
                                    pattern=[[-1, S]], channel_multiplier=1).then_inc(rel_ready, 1)
            pool.wait_ge(rel_ready, 1)
            pool.wait_ge(tables_ready, 1)

            def inverse_root(base_eps, target, eps_t, source, eps, n, name_eps, name_out):
                nc.gpsimd.tensor_tensor(eps_t, source, eps, ALU.add).then_inc(sems[name_eps], 1)
                pool.wait_ge(sems[name_eps], base_eps + 1)
                nc.gpsimd.tensor_tensor(target, eps_t, minus_half[:, 0:n], ALU.pow).then_inc(sems[name_out], 1)

            def layer_norm(at):
                half = NT // 2
                for i in range(2):
                    r = slice(i * half, (i + 1) * half)
                    pool.wait_ge(sems["ln_moments"], at("ln_moments") + half * (i + 1))
                    inverse_root(at("ln_var_eps") + i, rstd[:, r], var_eps[:, r], moments[:, r, 1], ln_eps[:], half,
                                 "ln_var_eps", "ln_rstd")

            with pool.Fori(0, NB) as b:
                layer_norm(lambda name: ln_at(name, b))

                def run(plan, at, start, g):
                    def inv_q(s):
                        n = at("q_sum_eps") + s - 2
                        pool.wait_ge(sems["q_squares"], at("q_squares") + s - 1)
                        inverse_root(n, q_inv_t[:], q_sum_eps_t[:], q_sum[:], rms_eps[:, 0:G], G, "q_sum_eps", "q_inv")

                    def inv_k():
                        pool.wait_ge(sems["kv_squares"], start("kv_squares") + NT // 2)
                        inverse_root(start("k_sum_eps"), k_inv_t[:], k_sum_eps_t[:], k_sum[:], rms_eps[:], NT,
                                     "k_sum_eps", "k_inv")

                    def normalise(s, h):
                        L = (s + 1) * P
                        if h % 2 == 0:
                            pool.wait_ge(sems["p_inv"], at("p_inv") + 2 * s + h // 2 + 1)
                        row = probs[:, s % 2, h, 0:L]
                        nc.gpsimd.tensor_tensor(row, row, p_inv_t[:, s % 2, h:h + 1].to_broadcast((P, L)),
                                                ALU.mult).then_inc(sems["p_ready"], 1)

                    def table(h):
                        if h == 0:
                            pool.wait_ge(sems["turned"], start("turned") + 1)
                        if plan is GROUP:
                            pool.wait_ge(sems["s_max"], at("s_max") + (NT - 1) * G + h + 1)
                        nc.gpsimd.tensor_tensor(bias[:, h, :], rel[:],
                                                slope_row[:, bass.ds(g * G + h, 1)].to_broadcast((P, S)),
                                                ALU.mult).then_inc(sems["bias_ready"], 1)

                    def x_rstd(t):
                        pool.wait_ge(sems["ln_moments"], at("ln_moments") + t + 1)
                        inverse_root(at("ln_var_eps") + t, rstd[:, t:t + 1], var_eps[:, t:t + 1], moments[:, t, 1:2],
                                     ln_eps[:, 0:1], 1, "ln_var_eps", "ln_rstd")

                    follow({"x_rstd": x_rstd, "inv_q": inv_q, "inv_k": inv_k, "normalise": normalise, "table": table}, plan)

                run_plans(pool, run, b, True)

        @block.vector
        def _(dve):
            nc.vector.memset(minus_half[:], -0.5)
            nc.vector.memset(ln_eps[:], LN_EPS)
            nc.vector.memset(rms_eps[:], HD * RMS_EPS)
            for h in range(H):
                last = nc.vector.memset(slope_row[:, h:h + 1], float(slopes[h]))
            last.then_inc(tables_ready, 1)
            dve.wait_ge(small_loaded, 48)

            carriers = itertools.count()

            def alone():
                nc.vector.memset(scratch[:, next(carriers) % CARRIERS, :], 0.0)

            nc.vector.tensor_scalar(wk_scaled[:], wk_norm[:], math.sqrt(HD), None, ALU.mult).then_inc(wk_scaled_ready, 1)
            dve.wait_ge(wk_scaled_ready, 1)

            def layer_norm(at, ready):
                half = NT // 2

                def statistics(tiles):
                    for t in tiles:
                        ready(t)
                        nc.vector.bn_stats(stats[:, t, :], y[:, t, :]).then_inc(sems["ln_stats"], 1)

                def mean_variance(tiles):
                    for t in tiles:
                        dve.wait_ge(sems["ln_stats"], at("ln_stats") + t + 1)
                        alone()
                        nc.vector.bn_aggr(moments[:, t, :], stats[:, t, :]).then_inc(sems["ln_moments"], 1)

                def normalise(tiles):
                    dve.wait_ge(sems["ln_rstd"], at("ln_rstd") + tiles[0] // half + 1)
                    for t in tiles:
                        nc.vector.tensor_scalar(x_normed[:, t, :], y[:, t, :], moments[:, t, 0:1], rstd[:, t:t + 1],
                                                ALU.subtract, ALU.mult).then_inc(sems["xn_ready"], 1)

                first, second = range(half), range(half, NT)
                statistics(first)
                mean_variance(first)
                statistics(second)
                normalise(first)
                mean_variance(second)
                normalise(second)

            def low(base, unit, target, source, high, scale=None):
                dve.wait_ge(sems["hi_done"], base + unit + 1)
                if scale is None:
                    nc.vector.tensor_tensor(target, source, high.bitcast(F32), ALU.subtract).then_inc(sems["lo_done"], 1)
                else:
                    nc.vector.scalar_tensor_tensor(target, source, scale, high.bitcast(F32), ALU.mult,
                                                   ALU.subtract).then_inc(sems["lo_done"], 1)

            with dve.Fori(0, NB) as b:
                def x_ready(t):
                    dve.wait_ge(x_loaded[t], b * 16 + 16)

                layer_norm(lambda name: ln_at(name, b), x_ready)
                base = ln_at("hi_done", b)
                for t in range(NT):
                    cols = slice(t * P, (t + 1) * P)
                    low(base, t, xnT_lo[:, :, cols], turn_ps[t % RING][:].rearrange("p (c n) -> p c n", c=C),
                        xnT_hi[:, :, cols])

                def run(plan, at, start):
                    unit_of, high_of = units(plan), high_units(plan)
                    base = start("hi_done")

                    def turn(what, *which):
                        unit = unit_of[(what, *which)]
                        bank = turn_ps[unit % RING][:]
                        if what in ("x", "lora"):
                            t, = which
                            target = x_turned[:, t, :] if what == "x" else low_turned[:, t, :]
                            dve.wait_ge(sems["turned"], start("turned") + unit + 1)
                            nc.vector.tensor_copy(target, bank[:, 0:target.shape[1]]).then_inc(sems["lo_done"], 1)
                            return
                        unit = high_of[(what, *which)]
                        if what == "p":
                            r = piece(*which) % RING
                            low(base, unit, pT_lo[:, r, :], bank, pT_hi[:, r, :])
                        elif what == "q":
                            flat = "p h n -> p (h n)"
                            low(base, unit, qT_lo[:, which[0] % 2].rearrange(flat), bank, qT_hi[:, which[0] % 2].rearrange(flat),
                                wq_norm[:])
                        elif what == "k":
                            cols = slice(which[0] * 512, (which[0] + 1) * 512)
                            low(base, unit, kT_lo[:, cols], bank, kT_hi[:, cols], wk_scaled[:])
                        elif what == "wkv":
                            chunks = slice(2 * which[0], 2 * which[0] + 2)
                            low(base, unit, wkvT_lo[:, chunks, :].rearrange("p c n -> p (c n)"), bank,
                                wkvT_hi[:, chunks, :].rearrange("p c n -> p (c n)"))
                        elif what == "wq":
                            low(base, unit, wqT_lo[:, which[0], :], bank, wqT_hi[:, which[0], :])
                        elif what == "wo":
                            low(base, unit, woT_lo[:, which[0], :], bank, woT_hi[:, which[0], :])

                    def score_max(s, h):
                        n = s * G + h
                        L = (s + 1) * P
                        if s == 0:
                            dve.wait_ge(sems["bias_ready"], at("bias_ready") - G + h + 1)
                        dve.wait_ge(sems["s_full"], at("s_full") + n + 1)
                        alone()
                        at_col = scores_col(s, h)
                        nc.vector.tensor_tensor_reduce(
                            out=probs[:, s % 2, h, 0:L], in0=s_ps[:, at_col:at_col + L], in1=bias[:, h, S - L:S],
                            scale=-1.0, scalar=BIG, op0=ALU.add, op1=ALU.min,
                            accum_out=neg_max[:, s % 2, h:h + 1]).then_inc(sems["s_max"], 1)

                    def invert(s, i):
                        n = s * G + 2 * i + 1
                        dve.wait_ge(sems["p_exp"], at("p_exp") + n + 1)
                        nc.vector.reciprocal(p_inv_t[:, s % 2, 2 * i:2 * i + 2],
                                             p_sum[:, s % 2, 2 * i:2 * i + 2]).then_inc(sems["p_inv"], 1)

                    def norm_q(s):
                        dve.wait_ge(sems["q_inv"], at("q_inv") + s - 1)
                        nc.vector.tensor_tensor(qn[:], q_ps[:].rearrange("p (h d) -> p h d", h=G),
                                                q_inv_t[:].unsqueeze(2).to_broadcast((P, G, HD)),
                                                ALU.mult).then_inc(sems["q_normed"], 1)

                    def kv(i):
                        dve.wait_ge(sems["kv_squares"], start("kv_squares") + i + 1)
                        nc.vector.tensor_copy(kv_raw[:, 2 * i:2 * i + 2, :],
                                              s_ps[:, 512 * (i % 2):512 * (i % 2 + 1)].rearrange("p (t n) -> p t n", t=2))\
                            .then_inc(sems["kv_copied"], 1)

                    def norm_k():
                        dve.wait_ge(sems["kv_copied"], start("kv_copied") + NT // 2)
                        dve.wait_ge(sems["k_inv"], start("k_inv") + 1)
                        nc.vector.tensor_tensor(k_norm[:], kv_raw[:, :, 0:HD],
                                                k_inv_t[:].unsqueeze(2).to_broadcast((P, NT, HD)),
                                                ALU.mult).then_inc(sems["k_normed"], 1)

                    def split_v():
                        dve.wait_ge(sems["v_hi_done"], start("v_hi_done") + 1)
                        nc.vector.tensor_tensor(v_lo[:], kv_raw[:, :, HD:2 * HD], v_hi[:].bitcast(F32),
                                                ALU.subtract).then_inc(sems["v_lo_done"], 1)

                    def split_o(s):
                        dve.wait_ge(sems["o_hi"], at("o_hi") + s + 1)
                        nc.vector.tensor_tensor(oT_lo[:].rearrange("p h n -> p (h n)"), o_ps[:],
                                                oT_hi[:].rearrange("p h n -> p (h n)").bitcast(F32),
                                                ALU.subtract).then_inc(sems["o_lo"], 1)

                    def add_y(s):
                        dve.wait_ge(sems["y_full"], at("y_full") + s + 1)
                        nc.vector.tensor_tensor(y[:, s, :], y_ps[:], y[:, s, :], ALU.add).then_inc(sems["y_added"], 1)

                    def x_stats(t):
                        dve.wait_ge(sems["y_added"], at("y_added") + t + 1)
                        nc.vector.bn_stats(stats[:, t, :], y[:, t, :]).then_inc(sems["ln_stats"], 1)

                    def x_moments(t):
                        dve.wait_ge(sems["ln_stats"], at("ln_stats") + t + 1)
                        alone()
                        nc.vector.bn_aggr(moments[:, t, :], stats[:, t, :]).then_inc(sems["ln_moments"], 1)

                    def x_norm(t):
                        if t % G == 0:
                            tile = ("p", NT - 2 + t // G, NT - 2 + t // G)
                            dve.wait_ge(sems["turned"], start("turned") + unit_of[tile] + 1)
                        dve.wait_ge(sems["ln_rstd"], at("ln_rstd") + t + 1)
                        nc.vector.tensor_scalar(x_normed[:, t, :], y[:, t, :], moments[:, t, 0:1], rstd[:, t:t + 1],
                                                ALU.subtract, ALU.mult).then_inc(sems["xn_ready"], 1)

                    def f_max(t):
                        dve.wait_ge(sems["f_full"], at("f_full") + t + 1)
                        alone()
                        nc.vector.tensor_tensor_reduce(
                            out=f_logits[:, t, :], in0=s_ps[:, 512 * (t % 2) + P:512 * (t % 2) + P + NE], in1=br_row[:],
                            scale=-1.0, scalar=BIG, op0=ALU.add, op1=ALU.min,
                            accum_out=f_neg_max[:, t:t + 1]).then_inc(sems["f_max"], 1)

                    def f_inv(t):
                        dve.wait_ge(sems["f_exp"], at("f_exp") + t + 1)
                        nc.vector.reciprocal(f_inv_t[:, t:t + 1], f_sum[:, t:t + 1]).then_inc(sems["f_inv"], 1)

                    def f_gate(t):
                        dve.wait_ge(sems["f_inv"], at("f_inv") + t + 1)
                        nc.vector.tensor_scalar(f_gates[:, t, :], f_weights[:, t, :], f_inv_t[:, t:t + 1],
                                                NE * LORA_SCALING, ALU.mult, ALU.mult).then_inc(sems["f_gate"], 1)

                    def f_low(t):
                        dve.wait_ge(sems["f_gate"], at("f_gate") + t + 1)
                        nc.vector.tensor_tensor(low_gated[:, t, :].rearrange("p (h r) -> p h r", r=RK),
                                                s_ps[:, 512 * (t % 2):512 * (t % 2) + P].rearrange("p (h r) -> p h r", r=RK),
                                                f_gates[:, t, :].unsqueeze(2).to_broadcast((P, NE, RK)),
                                                ALU.mult).then_inc(sems["f_low"], 1)

                    def add_f(t):
                        dve.wait_ge(sems["f_out"], at("f_out") + t + 1)
                        nc.vector.tensor_tensor(y[:, t, :], q_ps[:], y[:, t, :], ALU.add).then_inc(sems["f_added"], 1)

                    follow({"low": turn, "max": score_max, "invert": invert, "norm_q": norm_q, "kv": kv, "norm_k": norm_k,
                            "split_v": split_v, "split_o": split_o, "add_y": add_y, "x_stats": x_stats,
                            "x_moments": x_moments, "x_norm": x_norm, "f_max": f_max, "f_inv": f_inv,
                            "f_gate": f_gate, "f_low": f_low, "add_f": add_f}, plan)

                run_plans(dve, run, b)

        @block.tensor
        def _(pe):
            def turn(base, unit, sources):
                if base is not None:
                    pe.wait_ge(sems["lo_done"], base + max(0, unit - RING + 1))
                width, rows = sources[0].shape[0], sources[0].shape[1]
                for i, source in enumerate(sources):
                    last = nc.tensor.transpose(turn_ps[unit % RING][0:rows, i * width:(i + 1) * width],
                                               source, ident[0:width, 0:width])
                last.then_inc(sems["turned"], 1)

            def split_product(target, pairs, start=True, stop=True):
                for i, ((a_hi, a_lo), (b_hi, b_lo)) in enumerate(pairs):
                    for k, (a, m) in enumerate(((a_hi, b_hi), (a_hi, b_lo), (a_lo, b_hi))):
                        last = nc.tensor.matmul(target, a, m, start=start and i == 0 and k == 0,
                                                stop=stop and i == len(pairs) - 1 and k == 2)
                return last

            pe.wait_ge(ident_ready, 1)
            pe.wait_ge(ffn_loaded, 48)
            turn(None, 0, [a_raw[:, c * P:(c + 1) * P] for c in range(C)])
            turn(None, 1, [wr_raw[:, c * P:(c + 1) * P] for c in range(C)])
            pe.wait_ge(b_sorted_ready, 1)
            turn(None, 2, [b_sorted[:, o].rearrange("p h r -> p (h r)") for o in range(C)])

            with pe.Fori(0, NB) as b:
                base = ln_at("lo_done", b)
                for t in range(NT):
                    pe.wait_ge(sems["xn_ready"], ln_at("xn_ready", b) + t + 1)
                    turn(base, t, [x_normed[:, t, c * P:(c + 1) * P] for c in range(C)])

                def run(plan, at, start, g):
                    unit_of = units(plan)
                    base = start("lo_done")
                    ready = b * NG + g + 1
                    def turn_what(what, *which):
                        unit = unit_of[(what, *which)]
                        if what == "p":
                            s, j = which
                            if j == 0:
                                pe.wait_ge(sems["p_ready"], at("p_ready") + (s + 1) * G)
                            sources = [probs[:, s % 2, h, j * P:(j + 1) * P] for h in range(G)]
                        elif what == "q":
                            pe.wait_ge(sems["q_normed"], at("q_normed") + which[0])
                            sources = [qn[:, h, :] for h in range(G)]
                        elif what == "k":
                            if which[0] == 0:
                                pe.wait_ge(sems["k_normed"], start("k_normed") + 1)
                            sources = [k_norm[:, t, :] for t in range(4 * which[0], 4 * which[0] + 4)]
                        elif what == "wkv":
                            if which[0] == 0:
                                pe.wait_ge(wkv_loaded, 32 * ready)
                            sources = [wkv_raw[:, m, c * P:(c + 1) * P]
                                       for c in (2 * which[0], 2 * which[0] + 1) for m in range(2)]
                        elif what == "wq":
                            if which[0] == 0:
                                pe.wait_ge(wq_loaded, 16 * ready)
                            sources = [wq_raw[:, h, which[0] * P:(which[0] + 1) * P] for h in range(G)]
                        elif what == "wo":
                            if which[0] == 0:
                                pe.wait_ge(wo_loaded, 16 * (ready if plan is LAST_GROUP else ready - 1))
                            sources = [wo_raw[:, c, which[0] * P:(which[0] + 1) * P] for c in range(C)]
                        elif what == "x":
                            pe.wait_ge(sems["xn_ready"], at("xn_ready") + which[0] + 1)
                            sources = [x_normed[:, which[0], c * P:(c + 1) * P] for c in range(C)]
                        elif what == "lora":
                            pe.wait_ge(sems["f_low"], at("f_low") + which[0] + 1)
                            sources = [low_gated[:, which[0], :]]
                        turn(base, unit, sources)

                    def q_part(s, c):
                        if c == 0:
                            if plan is PREPARE and s == NT:
                                pe.wait_ge(sems["lo_done"], base + unit_of["wq", C - 1] + 1)
                            elif plan is GROUP and s == NT:
                                pe.wait_ge(sems["lo_done"], base + unit_of["wq", C - 1] + 1)
                            if not (plan is PREPARE and s == NT):
                                pe.wait_ge(sems["q_normed"], at("q_normed") + s - 1)
                        tok = slice(s % NT * P, (s % NT + 1) * P)
                        last = split_product(q_ps[:], [((xnT_hi[:, c, tok], xnT_lo[:, c, tok]), (wqT_hi[:, c, :], wqT_lo[:, c, :]))],
                                             start=c == 0, stop=c == C - 1)
                        if c == C - 1:
                            last.then_inc(sems["q_full"], 1)

                    def scores(s, h):
                        L = (s + 1) * P
                        n = s * G + h
                        if h == 0 and s == 0:
                            pe.wait_ge(sems["lo_done"], base)
                        elif h == 0:
                            pe.wait_ge(sems["lo_done"], base + unit_of["q", s] + 1)
                        if L > 512:
                            pe.wait_ge(sems["s_max"], at("s_max") + n)
                        elif n >= 2:
                            pe.wait_ge(sems["s_max"], at("s_max") + n - 1)
                        col = scores_col(s, h)
                        edge = L if L <= 512 else 512 - col
                        for c, w in ((0, edge), (edge, L - edge)):
                            if w == 0:
                                continue
                            last = split_product(s_ps[:, col + c:col + c + w],
                                                 [((qT_hi[:, s % 2, h, :], qT_lo[:, s % 2, h, :]),
                                                   (kT_hi[:, c:c + w], kT_lo[:, c:c + w]))])
                        last.then_inc(sems["s_full"], 1)

                    def kv(i):
                        if i == 0 and plan is PREPARE:
                            pe.wait_ge(sems["lo_done"], base + unit_of["wkv", C // 2 - 1] + 1)
                        elif i == 0:
                            pe.wait_ge(sems["s_max"], at("s_max") + NT * G)
                        if i >= 2:
                            pe.wait_ge(sems["kv_copied"], start("kv_copied") + i - 1)
                        for t in range(2):
                            tok = slice((2 * i + t) * P, (2 * i + t + 1) * P)
                            col = 512 * (i % 2) + t * 2 * HD
                            last = split_product(s_ps[:, col:col + 2 * HD],
                                                 [((xnT_hi[:, c, tok], xnT_lo[:, c, tok]), (wkvT_hi[:, c, :], wkvT_lo[:, c, :]))
                                                  for c in range(C)])
                        last.then_inc(sems["kv_full"], 1)

                    def values(s, j):
                        if s == 0:
                            pe.wait_ge(sems["v_lo_done"], at("v_lo_done"))
                        r = piece(s, j) % RING
                        pe.wait_ge(sems["lo_done"], base + unit_of["p", s, j] + 1)
                        last = split_product(o_ps[:], [((v_hi[:, j, :], v_lo[:, j, :]), (pT_hi[:, r, :], pT_lo[:, r, :]))],
                                             start=j == 0, stop=j == s)
                        if j == s:
                            last.then_inc(sems["o_full"], 1)

                    def y_product(s):
                        pe.wait_ge(sems["o_lo"], at("o_lo") + s + 1)
                        if s == 0:
                            pe.wait_ge(sems["lo_done"], base + unit_of["wo", G - 1] + 1)
                        else:
                            pe.wait_ge(sems["y_added"], at("y_added") + s)
                        split_product(y_ps[:], [((oT_hi[:, h, :], oT_lo[:, h, :]), (woT_hi[:, h, :], woT_lo[:, h, :]))
                                                for h in range(G)]).then_inc(sems["y_full"], 1)

                    def logits(t):
                        pe.wait_ge(sems["lo_done"], base + unit_of["x", t] + 1)
                        if t == 0:
                            pe.wait_ge(sems["s_max"], at("s_max") + NT * G)
                        if t >= 2:
                            pe.wait_ge(sems["f_low"], at("f_low") + t - 1)
                        for c in range(C):
                            last = nc.tensor.matmul(s_ps[:, 512 * (t % 2):512 * (t % 2) + P + NE],
                                                    x_turned[:, t, c * P:(c + 1) * P], arT[:, c, :],
                                                    start=c == 0, stop=c == C - 1)
                        last.then_inc(sems["f_full"], 1)

                    def f_out(t):
                        pe.wait_ge(sems["lo_done"], base + unit_of["lora", t] + 1)
                        if t == 0:
                            pe.wait_ge(sems["q_normed"], at("q_normed") + NT - 1)
                        else:
                            pe.wait_ge(sems["f_added"], at("f_added") + t)
                        nc.tensor.matmul(q_ps[:], low_turned[:, t, :], bT[:], start=True, stop=True).then_inc(sems["f_out"], 1)

                    follow({"turn": turn_what, "q_part": q_part, "scores": scores, "kv": kv, "values": values,
                            "y": y_product, "logits": logits, "f_out": f_out}, plan)

                run_plans(pe, run, b, True)


_INS = ["L0_attn_x", "L0_attn_Wq", "L0_attn_Wk", "L0_attn_Wv", "L0_attn_Wo", "L0_attn_q_norm_w", "L0_attn_k_norm_w",
        "L0_ffn_A", "L0_ffn_B", "L0_ffn_Wr", "L0_ffn_br"]


def kernel(**inputs):
    import concourse.bacc as bacc
    from concourse.bass_utils import run_bass_kernel_spmd

    nc = bacc.Bacc("TRN2", target_bir_lowering=False, num_devices=1)
    arrays, args = {}, []
    for name in _INS:
        a = np.ascontiguousarray(inputs[name])
        arrays[f"in_{name}"] = a
        args.append(nc.dram_tensor(f"in_{name}", a.shape, mybir.dt.from_np(a.dtype), kind="ExternalInput").ap())
    shape = inputs["L0_attn_x"].shape
    args.append(nc.dram_tensor("out_0", shape, F32, kind="ExternalOutput").ap())
    attention_lora_block(nc, *args)
    return run_bass_kernel_spmd(nc, [arrays], core_ids=[0]).results[0]["out_0"]
```
